# Optimizing a Trainium2 kernel written in Bass

```python
import numpy as np
import jax
import jax.numpy as jnp

def _softmax(x, axis=-1):
    return jax.nn.softmax(x, axis=axis)

def _gelu(x):
    return jax.nn.gelu(x, approximate=True)

def _silu(x):
    return jax.nn.silu(x)

def _sigmoid(x):
    return jax.nn.sigmoid(x)

def _layernorm(x, axis=-1, eps=1e-05):
    m = jnp.mean(x, axis=axis, keepdims=True)
    v = jnp.var(x, axis=axis, keepdims=True)
    return (x - m) / jnp.sqrt(v + eps)

def _scatter_add(tgt, idx, src, axis=0):
    return tgt.at[idx].add(src)

def _segment_sum(src, seg, n):
    return jax.ops.segment_sum(src, seg, n)
kernel_name = 'mk_seq_preln_d4_jaxref_r8_50808b'

def setup_inputs(seed: int=0):
    np.random.seed(seed)
    _w = jnp.asarray

    def _L0_attn_setup():
        import jax, jax.numpy as jnp
        import numpy as np
        LN_EPS = 1e-05

        def _ssm_scan(x_ssm, A, Bm, C, reverse):
            Bb, L, di = x_ssm.shape
            ds = Bm.shape[1]

            def step(h, x_t):
                h = jnp.clip(h * A[None] + x_t[:, :, None] * Bm[None], -10.0, 10.0)
                y = jnp.einsum('bid,id->bi', h, C)
                return (h, y)
            h0 = jnp.zeros((Bb, di, ds), x_ssm.dtype)
            _, ys = jax.lax.scan(step, h0, jnp.swapaxes(x_ssm, 0, 1), reverse=reverse)
            return jnp.swapaxes(ys, 0, 1)
        key = jax.random.key(seed)
        ks = jax.random.split(key, 6)
        B, L, D = (4, 256, 128)
        d_state, expand = (16, 2)
        d_inner = D * expand
        x = jax.random.normal(ks[0], (B, L, D), jnp.float32)
        in_proj_w = jax.random.normal(ks[1], (d_inner * 2, D), jnp.float32) * np.float32(1.0 / np.sqrt(D))
        A_log = jax.random.normal(ks[2], (d_inner, d_state), jnp.float32)
        B_mat = jax.random.normal(ks[3], (d_inner, d_state), jnp.float32) * np.float32(1.0 / np.sqrt(d_state))
        C_mat = jnp.full((d_inner, d_state), 0.01, jnp.float32)
        out_proj_w = jax.random.normal(ks[4], (D, d_inner), jnp.float32) * np.float32(1.0 / np.sqrt(d_inner))
        ln_w = jnp.ones((D,), jnp.float32)
        ln_b = jnp.zeros((D,), jnp.float32)
        return {'x': x, 'in_proj_w': in_proj_w, 'A_log': A_log, 'B_mat': B_mat, 'C_mat': C_mat, 'out_proj_w': out_proj_w, 'ln_w': ln_w, 'ln_b': ln_b}
    _L0_attn_in = _L0_attn_setup()

    def _L0_ffn_setup():
        import jax, jax.numpy as jnp
        import numpy as np
        B, T, C = (4, 256, 128)
        E, H, K = (8, 256, 2)
        key = jax.random.key(seed)
        ks = jax.random.split(key, 7)
        s_in = 1.0 / np.sqrt(C)
        s_hid = 1.0 / np.sqrt(H)
        return {'x': jax.random.normal(ks[0], (B, T, C), dtype=jnp.float32), 'gate_w': jax.random.uniform(ks[1], (C, E), jnp.float32, -s_in, s_in), 'gate_b': jnp.zeros((E,), jnp.float32), 'w1': jax.random.uniform(ks[2], (E, C, H), jnp.float32, -s_in, s_in), 'b1': jax.random.uniform(ks[3], (E, H), jnp.float32, -s_in, s_in), 'w2': jax.random.uniform(ks[4], (E, H, C), jnp.float32, -s_hid, s_hid), 'b2': jax.random.uniform(ks[5], (E, C), jnp.float32, -s_hid, s_hid)}
    _L0_ffn_in = _L0_ffn_setup()

    def _L1_attn_setup():
        import jax, jax.numpy as jnp
        import numpy as np
        B, N, D = (2, 256, 128)
        H, DK, DV = (8, 128, 128)
        key = jax.random.key(seed)
        kx, kq, kk, kv = jax.random.split(key, 4)
        scale = 0.02
        x = jax.random.normal(kx, (B, N, D), dtype=jnp.float32)
        Wq = jax.random.normal(kq, (H, DK, D), dtype=jnp.float32) * scale
        Wk = jax.random.normal(kk, (H, DK, D), dtype=jnp.float32) * scale
        Wv = jax.random.normal(kv, (H, DV, D), dtype=jnp.float32) * scale
        return {'x': x, 'Wq': Wq, 'Wk': Wk, 'Wv': Wv}
    _L1_attn_in = _L1_attn_setup()

    def _L1_ffn_setup():
        import jax, jax.numpy as jnp
        import numpy as np
        H = 128
        E = 64
        K = 8
        G = 8
        TOPK_GROUP = 4
        I_MOE = 64
        I_SHARED = 256
        SCALE = 2.5

        def relu2(x):
            return jnp.square(jax.nn.relu(x))

        def _route(xf, router_w, correction_bias):
            T = xf.shape[0]
            logits = xf @ router_w.T
            scores = jax.nn.sigmoid(logits)
            sfc = scores + correction_bias[None, :]
            grp = sfc.reshape(T, G, E // G)
            top2, _ = jax.lax.top_k(grp, 2)
            group_scores = top2.sum(-1)
            _, gidx = jax.lax.top_k(group_scores, TOPK_GROUP)
            gmask = jnp.zeros((T, G), sfc.dtype).at[jnp.arange(T)[:, None], gidx].set(1.0)
            emask = jnp.repeat(gmask, E // G, axis=1)
            masked = jnp.where(emask > 0, sfc, 0.0)
            _, tidx = jax.lax.top_k(masked, K)
            tw = jnp.take_along_axis(scores, tidx, axis=1)
            tw = tw / (tw.sum(-1, keepdims=True) + 1e-20)
            return (tidx, tw * SCALE)
        key = jax.random.key(seed)
        ks = jax.random.split(key, 7)
        x = jax.random.normal(ks[0], (2, 128, H), dtype=jnp.float32)
        router_w = jax.random.normal(ks[1], (E, H), dtype=jnp.float32) * 0.02
        correction_bias = jax.random.normal(ks[2], (E,), dtype=jnp.float32) * 0.01
        up_w = jax.random.normal(ks[3], (E, H, I_MOE), dtype=jnp.float32) * 0.02
        down_w = jax.random.normal(ks[4], (E, I_MOE, H), dtype=jnp.float32) * 0.02
        shared_up_w = jax.random.normal(ks[5], (H, I_SHARED), dtype=jnp.float32) * 0.02
        shared_down_w = jax.random.normal(ks[6], (I_SHARED, H), dtype=jnp.float32) * 0.02
        return {'x': x, 'router_w': router_w, 'correction_bias': correction_bias, 'up_w': up_w, 'down_w': down_w, 'shared_up_w': shared_up_w, 'shared_down_w': shared_down_w}
    _L1_ffn_in = _L1_ffn_setup()

    def _L2_attn_setup():
        import jax, jax.numpy as jnp
        import numpy as np
        D_MODEL = 128
        D_STATE = 16
        D_CONV = 4
        EXPAND = 2
        D_INNER = D_MODEL * EXPAND
        BATCH = 4
        SEQ_LEN = 512

        def _silu(v):
            return v * jax.nn.sigmoid(v)
        key = jax.random.key(seed)
        ks = jax.random.split(key, 6)

        def rn(k, shape, scale):
            return jax.random.normal(k, shape, dtype=jnp.float32) * scale
        x = rn(ks[0], (BATCH, SEQ_LEN, D_MODEL), 1.0)
        in_proj_w = rn(ks[1], (2 * D_INNER, D_MODEL), D_MODEL ** (-0.5))
        conv_w = rn(ks[2], (D_INNER, 1, D_CONV), D_CONV ** (-0.5))
        conv_b = rn(ks[3], (D_INNER,), 0.02)
        x_proj_w = rn(ks[4], (2 * D_STATE + 1, D_INNER), D_INNER ** (-0.5))
        A_log = jnp.log(jnp.arange(1, D_STATE + 1, dtype=jnp.float32))
        D = jnp.ones((D_INNER,), jnp.float32)
        out_proj_w = rn(ks[5], (D_MODEL, D_INNER), D_INNER ** (-0.5))
        return dict(x=x, in_proj_w=in_proj_w, conv_w=conv_w, conv_b=conv_b, x_proj_w=x_proj_w, A_log=A_log, D=D, out_proj_w=out_proj_w)
    _L2_attn_in = _L2_attn_setup()

    def _L2_ffn_setup():
        import math
        import jax, jax.numpy as jnp
        import numpy as np
        D_MODEL = 128
        D_FF = 512
        N_EXPERTS = 8
        CAPACITY_FACTOR = 1.25
        L, B = (64, 8)

        def _route(tokens, router_w):
            T = tokens.shape[0]
            E = router_w.shape[0]
            capacity = int(math.ceil(T / E * CAPACITY_FACTOR))
            logits = tokens @ router_w.T
            probs = jax.nn.softmax(logits, axis=-1)
            top1_idx = jnp.argmax(probs, axis=-1)
            top1_prob = jnp.max(probs, axis=-1)
            order = jnp.lexsort((-top1_prob, top1_idx))
            sorted_e = top1_idx[order]
            counts = jnp.bincount(top1_idx, length=E)
            start = jnp.cumsum(counts) - counts
            pos_in_group = jnp.arange(T) - start[sorted_e]
            keep_sorted = pos_in_group < capacity
            keep = jnp.zeros((T,), bool).at[order].set(keep_sorted)
            return jnp.where(keep, top1_idx, 0).astype(jnp.int32)
        key = jax.random.key(seed)
        ks = jax.random.split(key, 6)
        s_in = 1.0 / math.sqrt(D_MODEL)
        s_ff = 1.0 / math.sqrt(D_FF)
        return {'x': jax.random.normal(ks[0], (L, B, D_MODEL), dtype=jnp.float32), 'router_w': jax.random.uniform(ks[1], (N_EXPERTS, D_MODEL), minval=-s_in, maxval=s_in), 'W1': jax.random.uniform(ks[2], (N_EXPERTS, D_MODEL, D_FF), minval=-s_in, maxval=s_in), 'b1': jax.random.uniform(ks[3], (N_EXPERTS, D_FF), minval=-s_in, maxval=s_in), 'W2': jax.random.uniform(ks[4], (N_EXPERTS, D_FF, D_MODEL), minval=-s_ff, maxval=s_ff), 'b2': jax.random.uniform(ks[5], (N_EXPERTS, D_MODEL), minval=-s_ff, maxval=s_ff)}
    _L2_ffn_in = _L2_ffn_setup()

    def _L3_attn_setup():
        import jax, jax.numpy as jnp
        import numpy as np
        from jax import lax
        N_HEAD = 16
        D_HEAD = 64
        D_MODEL = 128
        N_ROLL = 2
        EPS = 1e-05
        LN_EPS = 1e-05
        SCALE = 1.0 / float(np.sqrt(D_HEAD))
        SLEN, BSZ = (256, 8)

        def _mul_roll_repeat(x):
            return jnp.concatenate([x * jnp.roll(x, i, axis=-1) for i in range(1, N_ROLL + 1)], axis=-1)
        key = jax.random.key(seed)
        k1, k2, k3 = jax.random.split(key, 3)
        h = jax.random.normal(k1, (SLEN, BSZ, D_MODEL), dtype=jnp.float32)
        W_qkvb = jax.random.normal(k2, (N_HEAD * (3 * D_HEAD + 1), D_MODEL), dtype=jnp.float32) * 0.02
        W_o = jax.random.normal(k3, (D_MODEL, N_HEAD * D_HEAD), dtype=jnp.float32) * 0.02
        ln_g = jnp.ones((D_MODEL,), dtype=jnp.float32)
        ln_b = jnp.zeros((D_MODEL,), dtype=jnp.float32)
        return {'h': h, 'W_qkvb': W_qkvb, 'W_o': W_o, 'ln_g': ln_g, 'ln_b': ln_b}
    _L3_attn_in = _L3_attn_setup()

    def _L3_ffn_setup():
        import jax, jax.numpy as jnp
        import numpy as np
        SINKHORN_ITERS = 8
        TEMPERATURE = 1.0
        EPS = 1e-06

        def sinkhorn(t):
            t = jnp.log(jnp.clip(t, EPS)) / TEMPERATURE
            for _ in range(SINKHORN_ITERS):
                t = t - jax.nn.logsumexp(t, axis=-2, keepdims=True)
                t = t - jax.nn.logsumexp(t, axis=-1, keepdims=True)
            return jnp.exp(t)
        key = jax.random.key(seed)
        k1, k2, k3 = jax.random.split(key, 3)
        B, N, D, E = (4, 512, 128, 8)
        x = jax.random.normal(k1, (B, N, D), dtype=jnp.float32)
        gate_w = jax.random.normal(k2, (D, E), dtype=jnp.float32) * D ** (-0.5)
        experts = jax.random.normal(k3, (E, D, D), dtype=jnp.float32) * D ** (-0.5)
        return {'x': x, 'gate_w': gate_w, 'experts': experts}
    _L3_ffn_in = _L3_ffn_setup()
    _d = {'L0_attn_x': _L0_attn_in['x'], 'L0_attn_in_proj_w': _L0_attn_in['in_proj_w'], 'L0_attn_A_log': _L0_attn_in['A_log'], 'L0_attn_B_mat': _L0_attn_in['B_mat'], 'L0_attn_C_mat': _L0_attn_in['C_mat'], 'L0_attn_out_proj_w': _L0_attn_in['out_proj_w'], 'L0_attn_ln_w': _L0_attn_in['ln_w'], 'L0_attn_ln_b': _L0_attn_in['ln_b'], 'L0_ffn_gate_w': _L0_ffn_in['gate_w'], 'L0_ffn_gate_b': _L0_ffn_in['gate_b'], 'L0_ffn_w1': _L0_ffn_in['w1'], 'L0_ffn_b1': _L0_ffn_in['b1'], 'L0_ffn_w2': _L0_ffn_in['w2'], 'L0_ffn_b2': _L0_ffn_in['b2'], 'L1_attn_Wq': _L1_attn_in['Wq'], 'L1_attn_Wk': _L1_attn_in['Wk'], 'L1_attn_Wv': _L1_attn_in['Wv'], 'L1_ffn_router_w': _L1_ffn_in['router_w'], 'L1_ffn_correction_bias': _L1_ffn_in['correction_bias'], 'L1_ffn_up_w': _L1_ffn_in['up_w'], 'L1_ffn_down_w': _L1_ffn_in['down_w'], 'L1_ffn_shared_up_w': _L1_ffn_in['shared_up_w'], 'L1_ffn_shared_down_w': _L1_ffn_in['shared_down_w'], 'L2_attn_in_proj_w': _L2_attn_in['in_proj_w'], 'L2_attn_conv_w': _L2_attn_in['conv_w'], 'L2_attn_conv_b': _L2_attn_in['conv_b'], 'L2_attn_x_proj_w': _L2_attn_in['x_proj_w'], 'L2_attn_A_log': _L2_attn_in['A_log'], 'L2_attn_D': _L2_attn_in['D'], 'L2_attn_out_proj_w': _L2_attn_in['out_proj_w'], 'L2_ffn_router_w': _L2_ffn_in['router_w'], 'L2_ffn_W1': _L2_ffn_in['W1'], 'L2_ffn_b1': _L2_ffn_in['b1'], 'L2_ffn_W2': _L2_ffn_in['W2'], 'L2_ffn_b2': _L2_ffn_in['b2'], 'L3_attn_W_qkvb': _L3_attn_in['W_qkvb'], 'L3_attn_W_o': _L3_attn_in['W_o'], 'L3_attn_ln_g': _L3_attn_in['ln_g'], 'L3_attn_ln_b': _L3_attn_in['ln_b'], 'L3_ffn_gate_w': _L3_ffn_in['gate_w'], 'L3_ffn_experts': _L3_ffn_in['experts']}
    _x0 = _d['L0_attn_x']
    _d['L0_attn_x'] = jax.random.normal(jax.random.fold_in(jax.random.key(seed), 1), (4, 1024, 128), dtype=_x0.dtype)
    del _x0
    return _d

def reference(L0_attn_x, L0_attn_in_proj_w, L0_attn_A_log, L0_attn_B_mat, L0_attn_C_mat, L0_attn_out_proj_w, L0_attn_ln_w, L0_attn_ln_b, L0_ffn_gate_w, L0_ffn_gate_b, L0_ffn_w1, L0_ffn_b1, L0_ffn_w2, L0_ffn_b2, L1_attn_Wq, L1_attn_Wk, L1_attn_Wv, L1_ffn_router_w, L1_ffn_correction_bias, L1_ffn_up_w, L1_ffn_down_w, L1_ffn_shared_up_w, L1_ffn_shared_down_w, L2_attn_in_proj_w, L2_attn_conv_w, L2_attn_conv_b, L2_attn_x_proj_w, L2_attn_A_log, L2_attn_D, L2_attn_out_proj_w, L2_ffn_router_w, L2_ffn_W1, L2_ffn_b1, L2_ffn_W2, L2_ffn_b2, L3_attn_W_qkvb, L3_attn_W_o, L3_attn_ln_g, L3_attn_ln_b, L3_ffn_gate_w, L3_ffn_experts):

    def _L0_attn_ref(x, in_proj_w, A_log, B_mat, C_mat, out_proj_w, ln_w, ln_b):
        import jax, jax.numpy as jnp
        import numpy as np
        LN_EPS = 1e-05

        def _ssm_scan(x_ssm, A, Bm, C, reverse):
            Bb, L, di = x_ssm.shape
            ds = Bm.shape[1]

            def step(h, x_t):
                h = jnp.clip(h * A[None] + x_t[:, :, None] * Bm[None], -10.0, 10.0)
                y = jnp.einsum('bid,id->bi', h, C)
                return (h, y)
            h0 = jnp.zeros((Bb, di, ds), x_ssm.dtype)
            _, ys = jax.lax.scan(step, h0, jnp.swapaxes(x_ssm, 0, 1), reverse=reverse)
            return jnp.swapaxes(ys, 0, 1)
        mu = jnp.mean(x, axis=-1, keepdims=True)
        var = jnp.mean((x - mu) ** 2, axis=-1, keepdims=True)
        xn = (x - mu) * jax.lax.rsqrt(var + LN_EPS) * ln_w + ln_b
        x_proj = jnp.einsum('bld,ed->ble', xn, in_proj_w)
        x_ssm, gate = jnp.split(x_proj, 2, axis=-1)
        A = -jnp.clip(jnp.exp(A_log), -10.0, -0.01)
        out_f = _ssm_scan(x_ssm, A, B_mat, C_mat, reverse=False)
        out_b = _ssm_scan(x_ssm, A, B_mat, C_mat, reverse=True)
        out = (out_f + out_b) * 0.5 * jax.nn.silu(gate)
        return jnp.einsum('bli,di->bld', out, out_proj_w)

    def _L0_ffn_ref(x, gate_w, gate_b, w1, b1, w2, b2):
        import jax, jax.numpy as jnp
        import numpy as np
        B, T, C = (4, 256, 128)
        E, H, K = (8, 256, 2)
        b, t, c = x.shape
        xf = x.reshape(b * t, c)
        logits = xf @ gate_w + gate_b
        probs = jax.nn.softmax(logits, axis=-1)
        gates, expert_idx = jax.lax.top_k(probs, K)
        h = jax.nn.relu(jnp.einsum('nc,ech->neh', xf, w1) + b1)
        expert_out = jnp.einsum('neh,ehc->nec', h, w2) + b2
        onehot = jax.nn.one_hot(expert_idx, E, dtype=xf.dtype)
        weights = jnp.einsum('nk,nke->ne', gates, onehot)
        out = jnp.einsum('ne,nec->nc', weights, expert_out)
        return out.reshape(b, t, c)

    def _L1_attn_ref(x, Wq, Wk, Wv):
        import jax, jax.numpy as jnp
        import numpy as np
        B, N, D = (2, 256, 128)
        H, DK, DV = (8, 128, 128)
        n = x.shape[-2]
        Q = jnp.einsum('bnd,hed->bhne', x, Wq)
        K = jnp.einsum('bnd,hed->bhne', x, Wk)
        V = jnp.einsum('bnd,hvd->bhnv', x, Wv)
        scores = jnp.einsum('bhne,bhme->bhnm', Q, K)
        causal = jnp.tril(jnp.ones((n, n), dtype=bool))
        sim = jnp.where(causal, jax.nn.relu(scores), jnp.float32(0.0)) / jnp.float32(n)
        head_out = jnp.einsum('bhnm,bhmv->bnv', sim, V)
        return x + head_out

    def _L1_ffn_ref(x, router_w, correction_bias, up_w, down_w, shared_up_w, shared_down_w):
        import jax, jax.numpy as jnp
        import numpy as np
        H = 128
        E = 64
        K = 8
        G = 8
        TOPK_GROUP = 4
        I_MOE = 64
        I_SHARED = 256
        SCALE = 2.5

        def relu2(x):
            return jnp.square(jax.nn.relu(x))

        def _route(xf, router_w, correction_bias):
            T = xf.shape[0]
            logits = xf @ router_w.T
            scores = jax.nn.sigmoid(logits)
            sfc = scores + correction_bias[None, :]
            grp = sfc.reshape(T, G, E // G)
            top2, _ = jax.lax.top_k(grp, 2)
            group_scores = top2.sum(-1)
            _, gidx = jax.lax.top_k(group_scores, TOPK_GROUP)
            gmask = jnp.zeros((T, G), sfc.dtype).at[jnp.arange(T)[:, None], gidx].set(1.0)
            emask = jnp.repeat(gmask, E // G, axis=1)
            masked = jnp.where(emask > 0, sfc, 0.0)
            _, tidx = jax.lax.top_k(masked, K)
            tw = jnp.take_along_axis(scores, tidx, axis=1)
            tw = tw / (tw.sum(-1, keepdims=True) + 1e-20)
            return (tidx, tw * SCALE)
        B, S, Hd = x.shape
        xf = x.reshape(-1, Hd)
        T = xf.shape[0]
        tidx, tw = _route(xf.astype(jnp.float32), router_w, correction_bias)
        combine = jnp.zeros((T, E), xf.dtype).at[jnp.arange(T)[:, None], tidx].add(tw.astype(xf.dtype))

        def body(acc, ew):
            wu, wd, c = ew
            return (acc + c[:, None] * (relu2(xf @ wu) @ wd), None)
        routed, _ = jax.lax.scan(body, jnp.zeros_like(xf), (up_w, down_w, combine.T))
        shared = relu2(xf @ shared_up_w) @ shared_down_w
        return (routed + shared).reshape(B, S, Hd)

    def _L2_attn_ref(x, in_proj_w, conv_w, conv_b, x_proj_w, A_log, D, out_proj_w):
        import jax, jax.numpy as jnp
        import numpy as np
        D_MODEL = 128
        D_STATE = 16
        D_CONV = 4
        EXPAND = 2
        D_INNER = D_MODEL * EXPAND
        BATCH = 4
        SEQ_LEN = 512

        def _silu(v):
            return v * jax.nn.sigmoid(v)
        b, l, _ = x.shape
        xz = jnp.einsum('bld,ed->ble', x, in_proj_w)
        x_inner, z = jnp.split(xz, 2, axis=-1)
        xc = jnp.transpose(x_inner, (0, 2, 1))
        xc = jax.lax.conv_general_dilated(xc, conv_w, window_strides=(1,), padding=[(D_CONV - 1, 0)], feature_group_count=D_INNER, dimension_numbers=('NCH', 'OIH', 'NCH'))
        xc = xc + conv_b[None, :, None]
        x_conv = _silu(jnp.transpose(xc, (0, 2, 1)))
        x_dbl = jnp.einsum('bld,ed->ble', x_conv, x_proj_w)
        delta = jax.nn.softplus(x_dbl[..., 0])
        B_ssm = x_dbl[..., 1:D_STATE + 1]
        C_ssm = x_dbl[..., D_STATE + 1:]
        A = -jnp.exp(A_log)

        def step(h, inp):
            x_t, d_t, B_t, C_t = inp
            dA = jnp.exp(d_t[:, None, None] * A)
            dB = d_t[:, None, None] * B_t[:, None, :]
            h = h * dA + x_t[:, :, None] * dB
            y_t = jnp.einsum('bdn,bn->bd', h, C_t)
            return (h, y_t)
        h0 = jnp.zeros((b, D_INNER, D_STATE), x.dtype)
        xs = (jnp.swapaxes(x_conv, 0, 1), jnp.swapaxes(delta, 0, 1), jnp.swapaxes(B_ssm, 0, 1), jnp.swapaxes(C_ssm, 0, 1))
        _, ys = jax.lax.scan(step, h0, xs)
        y = jnp.swapaxes(ys, 0, 1)
        y = y + x_conv * D
        y = y * _silu(z)
        return jnp.einsum('bld,od->blo', y, out_proj_w)

    def _L2_ffn_ref(x, router_w, W1, b1, W2, b2):
        import math
        import jax, jax.numpy as jnp
        import numpy as np
        D_MODEL = 128
        D_FF = 512
        N_EXPERTS = 8
        CAPACITY_FACTOR = 1.25
        L, B = (64, 8)

        def _route(tokens, router_w):
            T = tokens.shape[0]
            E = router_w.shape[0]
            capacity = int(math.ceil(T / E * CAPACITY_FACTOR))
            logits = tokens @ router_w.T
            probs = jax.nn.softmax(logits, axis=-1)
            top1_idx = jnp.argmax(probs, axis=-1)
            top1_prob = jnp.max(probs, axis=-1)
            order = jnp.lexsort((-top1_prob, top1_idx))
            sorted_e = top1_idx[order]
            counts = jnp.bincount(top1_idx, length=E)
            start = jnp.cumsum(counts) - counts
            pos_in_group = jnp.arange(T) - start[sorted_e]
            keep_sorted = pos_in_group < capacity
            keep = jnp.zeros((T,), bool).at[order].set(keep_sorted)
            return jnp.where(keep, top1_idx, 0).astype(jnp.int32)
        Lx, Bx, D = x.shape
        T = Lx * Bx
        E = router_w.shape[0]
        tokens = x.reshape(T, D)
        final_e = _route(tokens, router_w)
        out = jnp.zeros_like(tokens)
        for e in range(E):
            h = jax.nn.relu(tokens @ W1[e] + b1[e])
            y = h @ W2[e] + b2[e]
            out = out + jnp.where((final_e == e)[:, None], y, 0.0)
        return out.reshape(Lx, Bx, D)

    def _L3_attn_ref(h, W_qkvb, W_o, ln_g, ln_b):
        import jax, jax.numpy as jnp
        import numpy as np
        from jax import lax
        N_HEAD = 16
        D_HEAD = 64
        D_MODEL = 128
        N_ROLL = 2
        EPS = 1e-05
        LN_EPS = 1e-05
        SCALE = 1.0 / float(np.sqrt(D_HEAD))
        SLEN, BSZ = (256, 8)

        def _mul_roll_repeat(x):
            return jnp.concatenate([x * jnp.roll(x, i, axis=-1) for i in range(1, N_ROLL + 1)], axis=-1)
        slen, bsz, _ = h.shape
        qkvb = jnp.einsum('sbm,om->sbo', h, W_qkvb).reshape(slen, bsz, N_HEAD, 3 * D_HEAD + 1)
        hq = qkvb[..., :D_HEAD]
        hk = qkvb[..., D_HEAD:2 * D_HEAD]
        hv = qkvb[..., 2 * D_HEAD:3 * D_HEAD]
        hb = jax.nn.sigmoid(qkvb[..., 3 * D_HEAD:])
        hq = jnp.transpose(hq, (1, 2, 0, 3))
        hk = jnp.transpose(hk, (1, 2, 0, 3))
        hv = jnp.transpose(hv, (1, 2, 0, 3))
        hb = jnp.transpose(hb, (1, 2, 0, 3))
        hk = jnp.concatenate([jax.nn.relu(hk), jax.nn.relu(-hk)], axis=-1)
        hq = jnp.concatenate([jax.nn.relu(hq), jax.nn.relu(-hq)], axis=-1)
        hk = _mul_roll_repeat(hk)
        hq = _mul_roll_repeat(hq)
        hk = hk / hk.sum(-1, keepdims=True)
        hq = hq / hq.sum(-1, keepdims=True)
        D = 2 * N_ROLL * D_HEAD
        denom_acc = jnp.cumsum(hk, axis=2)
        key_denom = jnp.concatenate([jnp.zeros((bsz, N_HEAD, 1, D), hk.dtype), denom_acc[:, :, :-1, :]], axis=2)
        key_denom = jnp.einsum('bhsd,bhsd->bhs', key_denom, hk)
        key_denom = jnp.concatenate([jnp.ones((bsz, N_HEAD, 1), hk.dtype), key_denom[:, :, 1:]], axis=2)[..., None]
        hb = hb * key_denom
        hk = hk / (key_denom + EPS)
        denominator = jnp.einsum('bhsd,bhsd->bhs', denom_acc, hq)[..., None]
        qs = jnp.moveaxis(hq, 2, 0)
        ks = jnp.moveaxis(hk, 2, 0)
        vs = jnp.moveaxis(hv, 2, 0)
        bs = jnp.moveaxis(hb, 2, 0)
        W0 = jnp.zeros((bsz, N_HEAD, D, D_HEAD), hq.dtype)

        def step(W, inp):
            q_t, k_t, v_t, b_t = inp
            v_old = jnp.einsum('bhd,bhdv->bhv', k_t, W)
            new_v = b_t * (v_t - v_old)
            W = W + jnp.einsum('bhd,bhv->bhdv', k_t, new_v)
            out_t = jnp.einsum('bhd,bhdv->bhv', q_t, W)
            return (W, out_t)
        _, outs = lax.scan(step, W0, (qs, ks, vs, bs))
        out = jnp.moveaxis(outs, 0, 2)
        out = SCALE * out / (denominator + EPS)
        layer_out = jnp.transpose(out, (2, 0, 1, 3)).reshape(slen, bsz, N_HEAD * D_HEAD)
        attn_out = jnp.einsum('sbi,oi->sbo', layer_out, W_o)
        x = h + attn_out
        mu = x.mean(-1, keepdims=True)
        var = ((x - mu) ** 2).mean(-1, keepdims=True)
        return (x - mu) / jnp.sqrt(var + LN_EPS) * ln_g + ln_b

    def _L3_ffn_ref(x, gate_w, experts):
        import jax, jax.numpy as jnp
        import numpy as np
        SINKHORN_ITERS = 8
        TEMPERATURE = 1.0
        EPS = 1e-06

        def sinkhorn(t):
            t = jnp.log(jnp.clip(t, EPS)) / TEMPERATURE
            for _ in range(SINKHORN_ITERS):
                t = t - jax.nn.logsumexp(t, axis=-2, keepdims=True)
                t = t - jax.nn.logsumexp(t, axis=-1, keepdims=True)
            return jnp.exp(t)
        B, N, D = x.shape
        E = gate_w.shape[-1]
        M = N // E
        gate_logits = jnp.einsum('bnd,de->bne', x, gate_w)
        competitive_gates = sinkhorn(gate_logits)
        vals, idx = jax.lax.top_k(jnp.swapaxes(competitive_gates, -1, -2), M)
        gate_values = jnp.swapaxes(vals, -1, -2)
        routed_indices = jnp.swapaxes(idx, -1, -2)
        b_idx = jnp.arange(B)[:, None, None]
        routed = x[b_idx, routed_indices]
        routed = jnp.transpose(routed, (2, 0, 1, 3))
        outputs = jnp.einsum('ebmd,edf->ebmf', routed, experts)
        outputs = outputs * jnp.transpose(gate_values, (2, 0, 1))[..., None]
        vals_bmed = jnp.transpose(outputs, (1, 2, 0, 3))
        routed_back = jnp.zeros_like(x).at[b_idx, routed_indices].set(vals_bmed)
        return routed_back
    x = L0_attn_x
    x = x + _L0_attn_ref(_layernorm(x, axis=-1), L0_attn_in_proj_w, L0_attn_A_log, L0_attn_B_mat, L0_attn_C_mat, L0_attn_out_proj_w, L0_attn_ln_w, L0_attn_ln_b)
    x = x + _L0_ffn_ref(_layernorm(x, axis=-1), L0_ffn_gate_w, L0_ffn_gate_b, L0_ffn_w1, L0_ffn_b1, L0_ffn_w2, L0_ffn_b2)
    x = x + _L1_attn_ref(_layernorm(x, axis=-1), L1_attn_Wq, L1_attn_Wk, L1_attn_Wv)
    x = x + _L1_ffn_ref(_layernorm(x, axis=-1), L1_ffn_router_w, L1_ffn_correction_bias, L1_ffn_up_w, L1_ffn_down_w, L1_ffn_shared_up_w, L1_ffn_shared_down_w)
    x = x + _L2_attn_ref(_layernorm(x, axis=-1), L2_attn_in_proj_w, L2_attn_conv_w, L2_attn_conv_b, L2_attn_x_proj_w, L2_attn_A_log, L2_attn_D, L2_attn_out_proj_w)
    x = x + _L2_ffn_ref(_layernorm(x, axis=-1), L2_ffn_router_w, L2_ffn_W1, L2_ffn_b1, L2_ffn_W2, L2_ffn_b2)
    x = x + _L3_attn_ref(_layernorm(x, axis=-1), L3_attn_W_qkvb, L3_attn_W_o, L3_attn_ln_g, L3_attn_ln_b)
    x = x + _L3_ffn_ref(_layernorm(x, axis=-1), L3_ffn_gate_w, L3_ffn_experts)
    return x

_drawn_inputs = setup_inputs


def setup_inputs(seed=0):
    import zlib

    import numpy as np

    out = dict(_drawn_inputs(seed))
    spreads = {'L0_attn_C_mat': (0.009999999776482582, 0.6),
     'L0_attn_ln_w': (1.0, 0.6),
     'L0_attn_ln_b': (0.0, 0.8),
     'L0_ffn_gate_b': (0.0, 0.1),
     'L2_attn_D': (1.0, 0.2),
     'L3_attn_ln_g': (1.0, 0.2),
     'L3_attn_ln_b': (0.0, 0.1)}
    factors = {'L1_attn_Wq': 2.689,
     'L1_attn_Wk': 2.859,
     'L1_attn_Wv': 2.922,
     'L1_ffn_router_w': 3.168,
     'L1_ffn_correction_bias': 4.459,
     'L1_ffn_up_w': 2.997,
     'L1_ffn_down_w': 2.987,
     'L2_attn_conv_b': 2.777,
     'L3_attn_W_qkvb': 5.331,
     'L3_attn_W_o': 6.285}
    for name, (base, spread) in spreads.items():
        noise = np.random.default_rng([zlib.crc32(name.encode()), seed]).standard_normal(out[name].shape)
        drawn = base * np.exp(spread * noise) if base else spread * noise
        out[name] = jnp.asarray(drawn.astype(out[name].dtype))
    for name, factor in factors.items():
        out[name] = (out[name] * factor).astype(out[name].dtype)
    return out
```

```python
import concourse.bass as bass
from concourse import mybir
from contextlib import ExitStack

F32 = mybir.dt.float32
BF16 = mybir.dt.bfloat16
U32 = mybir.dt.uint32
ALU = mybir.AluOpType
ACT = mybir.ActivationFunctionType
AX = mybir.AxisListType

P = 128
BATCH, SEQ, C = 4, 1024, 128
T = BATCH * SEQ
NT = T // P
GROUP = 512
NG = T // GROUP
TPG = GROUP // P
LN_EPS = 1e-5
LEAST = 2.0 ** -126
STAGES = ('L0a', 'L0f', 'L1a', 'L1f', 'L2a', 'L2f', 'L3a', 'L3f')


class Chain:

    def __init__(self, eng, sem, base=0):
        self.eng, self.sem, self.base, self.n = eng, sem, base, 0

    def link(self, ins):
        self.n += 1
        ins.then_inc(self.sem, 1)
        self.eng.wait_ge(self.sem, self.base + self.n)


def bcast(ap, n):
    return ap.unsqueeze(len(ap.shape)).to_broadcast(list(ap.shape) + [n])


class Stage:

    def __init__(self, nc, name):
        self.nc, self.name, self.ctx, self.sems = nc, name, ExitStack(), []

    def __enter__(self):
        return self

    def __exit__(self, *a):
        self.ctx.close()
        self.nc.clear_and_free_semaphores(self.sems)
        self.nc.all_engine_barrier()

    def sb(self, name, shape, dt=F32):
        return self.ctx.enter_context(self.nc.sbuf_tensor(f"{self.name}_{name}", shape, dt))

    def ps(self, name, shape=(P, 512), dt=F32):
        return self.ctx.enter_context(self.nc.psum_tensor(f"{self.name}_{name}", list(shape), dt))

    def sem(self, name):
        self.sems.append(self.nc.alloc_semaphore(f"{self.name}_{name}"))
        return self.sems[-1]


def layernorm(nc, X, XN, XT, ident, name, affine=None):
    with Stage(nc, name) as s:
        stats = s.sb("stats", [P, NT, 6])
        mean, var, tmp, rstd = (s.sb(n, [P, NT]) for n in ("mean", "var", "tmp", "rstd"))
        eps = s.sb("eps", [P, 1])
        aff = s.sb("aff", [P, 2])
        aff_in = s.sem("aff_in")
        tp = [s.ps(f"tp{k}") for k in range(2)]
        stats_done, var_ready, std_ready, rstd_ready, xn_ready, t_ready, t_copied = (s.sem(n) for n in (
            "stats_done", "var_ready", "std_ready", "rstd_ready", "xn_ready", "t_ready", "t_copied"))
        ch = s.sem("vector_chain")
        with nc.Block() as block:

            @block.vector
            def _(dve):
                c = Chain(dve, ch)
                nc.vector.memset(eps[:], LN_EPS).then_inc(stats_done, 1)
                for i in range(NT):
                    nc.vector.bn_stats(stats[:, i], X[:, i]).then_inc(stats_done, 1)
                dve.wait_ge(stats_done, NT + 1)
                nc.vector.tensor_tensor(mean[:], stats[:, :, 1], stats[:, :, 4], ALU.add).then_inc(ch, 1)
                nc.vector.tensor_tensor(tmp[:], stats[:, :, 1], stats[:, :, 4], ALU.subtract).then_inc(ch, 1)
                nc.vector.tensor_tensor(var[:], stats[:, :, 2], stats[:, :, 5], ALU.add).then_inc(ch, 1)
                dve.wait_ge(ch, 3)
                c.n = 3
                c.link(nc.vector.tensor_scalar(mean[:], mean[:], 0.5, None, ALU.mult))
                c.link(nc.vector.tensor_tensor(tmp[:], tmp[:], tmp[:], ALU.mult))
                c.link(nc.vector.tensor_scalar(tmp[:], tmp[:], 0.25, None, ALU.mult))
                nc.vector.scalar_tensor_tensor(var[:], var[:], 1.0 / C, tmp[:], ALU.mult, ALU.add).then_inc(var_ready, 1)
                dve.wait_ge(std_ready, 1)
                nc.vector.reciprocal(rstd[:], tmp[:]).then_inc(rstd_ready, 1)
                dve.wait_ge(rstd_ready, 1)
                for i in range(NT):
                    nc.vector.tensor_scalar(XN[:, i], X[:, i], mean[:, i:i + 1], rstd[:, i:i + 1],
                                            ALU.subtract, ALU.mult).then_inc(xn_ready, 1)

                dve.wait_ge(xn_ready, NT)

            @block.sync
            def _(sp):
                if affine:
                    for k in range(2):
                        sp.dma_start(aff[:, k:k + 1], affine[k].rearrange("(c a) -> c a", a=1)).then_inc(aff_in, 16)

            @block.tensor
            def _(pe):
                for i in range(NT if XT is not None else 0):
                    g, k = divmod(i, TPG)
                    pe.wait_ge(xn_ready, i + 1)
                    if k == 0 and g >= 2:
                        pe.wait_ge(t_copied, g - 1)
                    nc.tensor.transpose(tp[g % 2][:, k * P:(k + 1) * P], XN[:, i], ident[:]).then_inc(t_ready, 1)

            @block.scalar
            def _(act):
                act.wait_ge(var_ready, 1)
                nc.scalar.activation(tmp[:], var[:], ACT.Sqrt, bias=eps[:]).then_inc(std_ready, 1)
                if XT is None:
                    return
                if affine:
                    act.wait_ge(aff_in, 32)
                for g in range(NG):
                    act.wait_ge(t_ready, TPG * (g + 1))
                    dst = XT[:, g * GROUP:(g + 1) * GROUP]
                    if affine:
                        ins = nc.scalar.activation(dst, tp[g % 2][:], ACT.Identity, bias=aff[:, 1:2], scale=aff[:, 0:1])
                    else:
                        ins = nc.scalar.activation(dst, tp[g % 2][:], ACT.Copy)
                    ins.then_inc(t_copied, 1)
                act.wait_ge(t_copied, NG)


def descending_rank(nc, c, rank, tmp, v, n):
    c.link(nc.vector.memset(rank[:], 0.0))
    for j in range(n):
        other = v[:, :, j:j + 1]
        if j:
            c.link(nc.vector.tensor_tensor(tmp[:, :, :j], other.to_broadcast([P, v.shape[1], j]), v[:, :, :j], ALU.is_gt))
            c.link(nc.vector.tensor_tensor(rank[:, :, :j], rank[:, :, :j], tmp[:, :, :j], ALU.add))
        if j < n - 1:
            m = n - 1 - j
            c.link(nc.vector.tensor_tensor(tmp[:, :, j + 1:], other.to_broadcast([P, v.shape[1], m]), v[:, :, j + 1:], ALU.is_ge))
            c.link(nc.vector.tensor_tensor(rank[:, :, j + 1:], rank[:, :, j + 1:], tmp[:, :, j + 1:], ALU.add))
def mixer_clipped_scan(nc, X, XN, XT, ident, in_proj_w, A_log, B_mat, C_mat, out_proj_w, ln_w, ln_b):
    DI, DS = B_mat.shape
    CT = DI // P
    NSEG = 2 * CT
    BOUND = 10.0
    QUAD = 4
    layernorm(nc, XN, XN, XT, ident, "ln2", affine=(ln_w, ln_b))
    with Stage(nc, "mix") as s:
        wi = s.sb("wi", [P, 2 * CT, C])
        wiT = s.sb("wiT", [P, 2 * CT * P])
        wo = s.sb("wo", [P, DI])
        woT = s.sb("woT", [P, CT, C])
        al, B, Cm, absB, nCB, lim = (s.sb(n, [P, CT, DS]) for n in ("al", "B", "Cm", "absB", "nCB", "lim"))
        gain = s.sb("gain", [P, CT])
        decay = s.sb("decay", [P, 1])
        limS, nCBS = (s.sb(n, [P, NSEG, DS]) for n in ("limS", "nCBS"))
        d0 = s.sb("d0", [P, SEQ, 2])
        d1 = s.sb("d1", [P, SEQ, 2])
        q = s.sb("q", [P, SEQ, 2])
        xs, gate, y = (s.sb(n, [P, CT, SEQ]) for n in ("xs", "gate", "y"))
        S, G = (s.sb(n, [P, NSEG, SEQ]) for n in ("S", "G"))
        mx = s.sb("mx", [P, NSEG, 1])
        reach = s.sb("reach", [P, NSEG, DS])
        most = s.sb("most", [P, NSEG * DS])
        bit = s.sb("bit", [1, NSEG, DS])
        flags = s.sb("flags", [1, NSEG, DS])
        mask_f = s.sb("mask_f", [1, NSEG])
        masks = s.sb("masks", [1, NSEG], mybir.dt.int32)
        pj = [s.ps(f"pj{k}") for k in range(4)]
        po = [s.ps(f"po{k}") for k in range(2)]
        w_in, c_in, w_mm, w_copied, exp_ready, const_ready, pj_mm, x_copied, g_ready, y_ready = (s.sem(n) for n in (
            "w_in", "c_in", "w_mm", "w_copied", "exp_ready", "const_ready", "pj_mm", "x_copied", "g_ready", "y_ready"))
        reach_ready, most_ready, out_mm, x_added, ch, fix = (s.sem(n) for n in (
            "reach_ready", "most_ready", "out_mm", "x_added", "vector_chain", "fix"))
        apart = s.sem("apart")
        with nc.Block() as block:

            @block.sync
            def _(sp):
                sp.dma_start(wi[:], in_proj_w.rearrange("(k p) c -> p k c", p=P)).then_inc(w_in, 16)
                sp.dma_start(wo[:], out_proj_w).then_inc(w_in, 16)
                for dst, src in ((al, A_log), (B, B_mat), (Cm, C_mat)):
                    sp.dma_start(dst[:], src.rearrange("(k p) d -> p k d", p=P)).then_inc(c_in, 16)

            @block.tensor
            def _(pe):
                pe.wait_ge(w_in, 32)
                for k in range(2 * CT):
                    nc.tensor.transpose(pj[0][:, k * P:(k + 1) * P], wi[:, k], ident[:])
                for k in range(CT):
                    last = nc.tensor.transpose(pj[1][:, k * P:(k + 1) * P], wo[:, k * P:(k + 1) * P], ident[:])
                last.then_inc(w_mm, 1)
                pe.wait_ge(w_copied, 2)
                with pe.Fori(0, BATCH) as b:
                    for k in range(2 * CT):
                        for half in range(2):
                            n = k * 2 + half
                            if k < CT:
                                pe.wait_ge(g_ready, b * 4 + (n + 1))
                            else:
                                pe.wait_ge(x_copied, b * 4 + (n - 3))
                            nc.tensor.matmul(pj[n % 4][:], wiT[:, k * P:(k + 1) * P], XT[:, bass.ds(b * SEQ + half * GROUP, GROUP)],
                                             start=True, stop=True).then_inc(pj_mm, 1)
                    pe.wait_ge(y_ready, b + 1)
                    pe.wait_ge(x_added, b * 2 + 1)
                    for t in range(SEQ // P):
                        o = po[t // TPG][:, (t % TPG) * C:(t % TPG + 1) * C]
                        for k in range(CT):
                            ins = nc.tensor.matmul(o, y[:, k, t * P:(t + 1) * P], woT[:, k], start=(k == 0), stop=(k == CT - 1))
                    ins.then_inc(out_mm, 1)

            @block.scalar
            def _(act):
                act.wait_ge(c_in, 48)
                nc.scalar.activation(al[:], al[:], ACT.Exp).then_inc(exp_ready, 1)
                act.wait_ge(w_mm, 1)
                nc.scalar.activation(wiT[:], pj[0][:], ACT.Copy).then_inc(w_copied, 1)
                nc.scalar.activation(woT[:].rearrange("p k c -> p (k c)"), pj[1][:, 0:CT * P], ACT.Copy).then_inc(w_copied, 1)
                act.sem_inc(g_ready, 4)
                with act.Fori(0, BATCH) as b:
                    for n in range(8):
                        k, half = divmod(n, 2)
                        act.wait_ge(pj_mm, b * 8 + (n + 1))
                        act.wait_ge(y_ready, b)
                        if k < CT:
                            nc.scalar.activation(xs[:, k, half * GROUP:(half + 1) * GROUP], pj[n % 4][:], ACT.Copy).then_inc(x_copied, 1)
                        else:
                            nc.scalar.activation(gate[:, k - CT, half * GROUP:(half + 1) * GROUP], pj[n % 4][:], ACT.Silu).then_inc(g_ready, 1)

            @block.gpsimd
            def _(pool):
                with pool.Fori(0, BATCH) as b:
                    pool.wait_ge(reach_ready, b + 1)
                    pool.sem_inc(apart, 1)
                    nc.gpsimd.partition_all_reduce(most[:], reach[:].rearrange("p s d -> p (s d)"), P, bass.bass_isa.ReduceOp.max).then_inc(most_ready, 1)

            @block.vector
            def _(dve):
                c = Chain(dve, ch)
                tt, ts, stt, redu = nc.vector.tensor_tensor, nc.vector.tensor_scalar, nc.vector.scalar_tensor_tensor, nc.vector.tensor_reduce
                dve.wait_ge(c_in, 48)
                dve.wait_ge(exp_ready, 1)
                c.link(ts(al[:], al[:], -BOUND, -0.01, ALU.max, ALU.min))
                c.link(ts(decay[:], al[:, 0, 0:1], -1.0, None, ALU.mult))
                c.link(ts(d0[:, :, 0], al[:, 0, 0:1].to_broadcast([P, SEQ]), 1.0, None, ALU.mult))
                c.link(nc.vector.memset(d0[:, :, 1], -1.0))
                c.link(stt(nCB[:], Cm[:], -0.5, B[:], ALU.mult, ALU.mult))
                c.link(redu(gain[:], nCB[:], AX.X, ALU.add))
                c.link(ts(gain[:], gain[:], -1.0, None, ALU.mult))
                c.link(ts(absB[:], B[:], -1.0, None, ALU.mult))
                c.link(tt(absB[:], absB[:], B[:], ALU.max))
                c.link(ts(lim[:], absB[:], 1e-30, None, ALU.max))
                c.link(nc.vector.reciprocal(lim[:], lim[:]))
                for dr in range(2):
                    c.link(ts(limS[:, dr * CT:(dr + 1) * CT], lim[:], BOUND, None, ALU.mult))
                    c.link(nc.vector.tensor_copy(nCBS[:, dr * CT:(dr + 1) * CT], nCB[:]))
                for d in range(DS):
                    last = nc.vector.memset(bit[:, :, d:d + 1], float(1 << d))
                c.link(last)
                dve.sem_inc(x_added, 1)

                def correct(b, k, d):
                    n = k * DS + d
                    done = (b * (NSEG * DS) + n) * 5
                    sk = S[:, bass.ds(k, 1), :].rearrange("p a t -> p (a t)")
                    gk = G[:, bass.ds(k, 1), :].rearrange("p a t -> p (a t)")
                    L = limS[:].rearrange("p k d -> p (k d)")[:, bass.ds(n, 1)]
                    w = nCBS[:].rearrange("p k d -> p (k d)")[:, bass.ds(n, 1)]
                    ts(d1[:, :, 0], sk, -1.0, L, ALU.mult, ALU.add).then_inc(fix, 1)
                    ts(d1[:, :, 1], sk, L, None, ALU.add).then_inc(fix, 1)
                    dve.wait_ge(fix, done + 2)
                    nc.vector.tensor_tensor_scan(q[:].rearrange("p t a -> p (t a)"), d0[:].rearrange("p t a -> p (t a)"),
                                                 d1[:].rearrange("p t a -> p (t a)"), 0.0, ALU.mult, ALU.min).then_inc(fix, 1)
                    dve.wait_ge(fix, done + 3)
                    stt(gk, q[:, :, 1], w, gk, ALU.mult, ALU.add).then_inc(fix, 1)
                    dve.wait_ge(fix, done + 4)
                    dve.sem_inc(fix, 1)

                base = c.n
                LINKS = NSEG + 4 + NSEG + 2 * CT - 1
                with dve.Fori(0, BATCH) as b:
                    cc = Chain(dve, ch, base + b * LINKS)
                    dve.wait_ge(x_copied, b * 4 + 4)
                    for k in range(NSEG):
                        dr, ct = divmod(k, CT)
                        src = xs[:, ct] if dr == 0 else xs[:, ct, ::-1]
                        cc.link(nc.vector.tensor_tensor_scan(S[:, k], decay[:].to_broadcast([P, SEQ]), src, 0.0, ALU.mult, ALU.add))
                    cc.link(redu(mx[:], S[:], AX.X, ALU.max, apply_absolute_value=True))
                    for dr in range(2):
                        last = tt(reach[:, dr * CT:(dr + 1) * CT], absB[:], mx[:, dr * CT:(dr + 1) * CT].to_broadcast([P, CT, DS]), ALU.mult)
                    last.then_inc(reach_ready, 1)
                    for k in range(NSEG):
                        cc.link(ts(G[:, k], S[:, k], gain[:, k % CT:k % CT + 1], None, ALU.mult))
                    dve.wait_ge(most_ready, b + 1)
                    cc.link(stt(flags[:], most[0:1].rearrange("p (s d) -> p s d", d=DS), BOUND * 0.999, bit[:], ALU.is_gt, ALU.mult))
                    cc.link(redu(mask_f[:], flags[:], AX.X, ALU.add))
                    cc.link(nc.vector.tensor_copy(masks[:], mask_f[:]))
                    dve.sem_inc(apart, 1)
                    with dve.Fori(0, NSEG) as k:
                        mask = dve.value_load(masks[0:1, bass.ds(k, 1)], min_val=0, max_val=2 ** DS - 1)
                        for quad in range(DS // QUAD):
                            with dve.If((mask & (((1 << QUAD) - 1) << (quad * QUAD))) > 0):
                                for d in range(quad * QUAD, (quad + 1) * QUAD):
                                    with dve.If((mask & (1 << d)) > 0):
                                        correct(b, k, d)
                                    with dve.Else():
                                        dve.sem_inc(fix, 5)
                                dve.sem_inc(apart, 1)
                            with dve.Else():
                                dve.sem_inc(fix, 5 * QUAD)
                    dve.wait_ge(g_ready, b * 4 + 8)
                    for ct in range(CT):
                        cc.link(tt(y[:, ct], G[:, ct], G[:, CT + ct, ::-1], ALU.add))
                        ins = tt(y[:, ct], y[:, ct], gate[:, ct], ALU.mult)
                        if ct < CT - 1:
                            cc.link(ins)
                        else:
                            ins.then_inc(y_ready, 1)
                    assert cc.n == LINKS, cc.n
                    dve.wait_ge(out_mm, b + 1)
                    for half in range(2):
                        xt = X[:, bass.ds(b * (SEQ // P) + half * TPG, TPG), :]
                        tt(xt, po[half][:].rearrange("p (t c) -> p t c", c=C), xt, ALU.add).then_inc(x_added, 1)
                dve.wait_ge(x_added, 2 * BATCH + 1)
def moe_top2(nc, X, XN, XT, ident, gate_w, gate_b, w1, b1, w2, b2):
    E, H = w1.shape[0], w1.shape[2]
    HT = H // P
    with Stage(nc, "moe2") as s:
        gw = s.sb("gw", [P, E])
        gb = s.sb("gb", [P, E])
        w1s = s.sb("w1s", [P, E, H])
        b1s = s.sb("b1s", [P, E * HT])
        w2s = s.sb("w2s", [P, E * HT, C])
        b2s = s.sb("b2s", [E, C])
        lg, ex, rank, tmp = (s.sb(n, [P, NT, E]) for n in ("lg", "ex", "rank", "tmp"))
        red = s.sb("red", [P, NT, 1])
        wT = s.sb("wT", [E, T])
        wTg = s.sb("wTg", [E, 2, GROUP])
        hid = s.sb("hid", [P, 2, E * HT, GROUP])
        pb = [s.ps(f"pb{k}") for k in range(2)]
        pl = pb[0][:, 0:NT * E]
        ph = [s.ps(f"ph{k}") for k in range(2)]
        po = [[s.ps(f"po{k}{h}") for h in range(2)] for k in range(2)]
        loaded, gates_in, w1_in, logits_ready, sm_shift, sm_exp, w_ready, wt_ready, wt_copied = (s.sem(n) for n in (
            "loaded", "gates_in", "w1_in", "logits_ready", "sm_shift", "sm_exp", "w_ready", "wt_ready", "wt_copied"))
        wg_ready, hid_mm, hid_ready, out_mm, out_used, ch = (s.sem(n) for n in (
            "wg_ready", "hid_mm", "hid_ready", "out_mm", "out_used", "vector_chain"))
        with nc.Block() as block:

            @block.sync
            def _(sp):
                sp.dma_start(gw[:], gate_w).then_inc(gates_in, 16)
                sp.dma_start(gb[:], gate_b.rearrange("(a e) -> a e", a=1).to_broadcast([P, E])).then_inc(gates_in, 16)
                sp.dma_start(w1s[:], w1.rearrange("e c h -> c e h")).then_inc(w1_in, 16)
                sp.dma_start(b1s[:], b1.rearrange("e (k p) -> p (e k)", p=P)).then_inc(w1_in, 16)
                sp.dma_start(w2s[:], w2.rearrange("e (k p) c -> p (e k) c", p=P)).then_inc(loaded, 16)
                sp.dma_start(b2s[:], b2).then_inc(loaded, 16)

            @block.tensor
            def _(pe):
                pe.wait_ge(gates_in, 32)
                for i in range(NT):
                    last = nc.tensor.matmul(pl[:, i * E:(i + 1) * E], XT[:, i * P:(i + 1) * P], gw[:], start=True, stop=True)
                last.then_inc(logits_ready, 1)
                pe.wait_ge(w_ready, 1)
                for i in range(NT):
                    g, k = divmod(i, TPG)
                    if k == 0 and g >= 2:
                        pe.wait_ge(wt_copied, g - 1)
                    nc.tensor.transpose(ph[g % 2][0:E, k * P:(k + 1) * P], lg[:, i], ident[:]).then_inc(wt_ready, 1)
                pe.wait_ge(w1_in, 32)
                pe.wait_ge(loaded, 32)
                pe.wait_ge(wt_copied, NG)
                NH = E * HT
                pe.sem_inc(out_mm, TPG + 1)
                with pe.Fori(0, NG // 2) as g2:
                    for par in range(2):
                        g = g2 * 2 + par
                        for j in range(NH):
                            pe.wait_ge(hid_ready, g * NH + (j + 1))
                            nc.tensor.matmul(ph[j % 2][:], w1s[:, j // HT, (j % HT) * P:(j % HT + 1) * P],
                                             XT[:, bass.ds(g * GROUP, GROUP)], start=True, stop=True).then_inc(hid_mm, 1)
                        pe.wait_ge(hid_ready, g * NH + NH + 2)
                        pe.wait_ge(wg_ready, g + 1)
                        for t in range(TPG):
                            pe.wait_ge(out_used, g * TPG + t + 1)
                            for e in range(E):
                                o = po[t % 2][e // 4][:, (e % 4) * C:(e % 4 + 1) * C]
                                for k in range(HT):
                                    nc.tensor.matmul(o, hid[:, par, e * HT + k, t * P:(t + 1) * P], w2s[:, e * HT + k, :],
                                                     start=(k == 0), stop=(k == HT - 1))
                            nc.tensor.matmul(pb[t % 2][:, 0:C], wTg[:, par, t * P:(t + 1) * P], b2s[:],
                                             start=True, stop=True).then_inc(out_mm, 1)

            @block.scalar
            def _(act):
                act.wait_ge(sm_shift, 1)
                nc.scalar.activation(ex[:], lg[:], ACT.Exp).then_inc(sm_exp, 1)
                for g in range(NG):
                    act.wait_ge(wt_ready, TPG * (g + 1))
                    nc.scalar.activation(wT[:, g * GROUP:(g + 1) * GROUP], ph[g % 2][0:E, :], ACT.Copy).then_inc(wt_copied, 1)
                act.wait_ge(w1_in, 32)
                act.sem_inc(hid_ready, 2)
                NH = E * HT
                with act.Fori(0, NG // 2) as g2:
                    for par in range(2):
                        g = g2 * 2 + par
                        for j in range(NH):
                            act.wait_ge(hid_mm, g * NH + (j + 1))
                            if j == 0:
                                act.wait_ge(out_mm, g * TPG + 1)
                            nc.scalar.activation(hid[:, par, j], ph[j % 2][:], ACT.Relu, bias=b1s[:, j:j + 1]).then_inc(hid_ready, 1)

            @block.vector
            def _(dve):
                c = Chain(dve, ch)
                dve.wait_ge(gates_in, 32)
                dve.wait_ge(logits_ready, 1)
                plv = pl.rearrange("p (t e) -> p t e", e=E)
                c.link(nc.vector.tensor_tensor(lg[:], plv, gb[:].unsqueeze(1).to_broadcast([P, NT, E]), ALU.add))
                c.link(nc.vector.tensor_reduce(red[:], lg[:], AX.X, ALU.max))
                nc.vector.tensor_tensor(lg[:], lg[:], red[:].to_broadcast([P, NT, E]), ALU.subtract).then_inc(sm_shift, 1)
                dve.wait_ge(sm_exp, 1)
                descending_rank(nc, c, rank, tmp, ex, E)
                c.link(nc.vector.tensor_reduce(red[:], ex[:], AX.X, ALU.add))
                c.link(nc.vector.reciprocal(red[:], red[:]))
                c.link(nc.vector.tensor_tensor(ex[:], ex[:], red[:].to_broadcast([P, NT, E]), ALU.mult))
                nc.vector.scalar_tensor_tensor(lg[:], rank[:], 1.5, ex[:], ALU.is_lt, ALU.mult).then_inc(w_ready, 1)
                dve.wait_ge(w_ready, 1)
                dve.wait_ge(wt_copied, NG)
                dve.sem_inc(out_used, 2)
                base = c.n
                with dve.Fori(0, NG // 2) as g2:
                    for par in range(2):
                        g = g2 * 2 + par
                        dve.wait_ge(out_mm, g * TPG + 1)
                        nc.vector.tensor_copy(wTg[:, par], wT[:, bass.ds(g * GROUP, GROUP)]).then_inc(wg_ready, 1)
                        for t in range(TPG):
                            i = g * TPG + t
                            dve.wait_ge(out_mm, g * TPG + (t + TPG + 2))
                            cc = Chain(dve, ch, base + (g * TPG + t) * E)
                            xt = X[:, bass.ds(i, 1), :]
                            cc.link(nc.vector.tensor_tensor(xt, pb[t % 2][:, 0:C].unsqueeze(1), xt, ALU.add))
                            for e in range(E):
                                o = po[t % 2][e // 4][:, (e % 4) * C:(e % 4 + 1) * C].unsqueeze(1)
                                ins = nc.vector.scalar_tensor_tensor(xt, o, lg[:, bass.ds(i, 1), e:e + 1].rearrange("p a b -> p (a b)"), xt, ALU.mult, ALU.add)
                                if e < E - 1:
                                    cc.link(ins)
                                else:
                                    ins.then_inc(out_used, 1)
                            dve.wait_ge(out_used, i + 3)
def relu_attention(nc, X, XN, XT, ident, Wq, Wk, Wv):
    H = Wq.shape[0]
    KT = SEQ // P
    full = [(1, m, GROUP, GROUP, False) for m in range(TPG)]
    diag = [(m // TPG, m, m * P, GROUP - (m % TPG) * P, True) for m in range(KT)]
    BLOCKS = [b for pair in zip(diag[:TPG], full) for b in pair] + diag[TPG:]
    NB, ND, NF = len(BLOCKS), len(diag), len(full)
    SC = 4
    with Stage(nc, "attn") as s:
        wq, wk, wv = (s.sb(n, [P, H, C]) for n in ("wq", "wk", "wv"))
        wqk = s.sb("wqk", [P, H, C])
        wvT = s.sb("wvT", [P, H, C])
        wqk_f = s.sb("wqk_f", [P, 2, C])
        mask = s.sb("mask", [P, GROUP])
        xb = s.sb("xb", [P, SEQ])
        zeros = s.sb("zeros", [P, GROUP], BF16)
        q = s.sb("q", [P, 2, SEQ])
        v = s.sb("v", [P, 2, KT, C])
        sim = s.sb("sim", [P, 2, NB, GROUP])
        o = s.sb("o", [P, SEQ])
        sc = [s.ps(f"sc{k}") for k in range(SC)]
        qp = [s.ps(f"qp{k}") for k in range(2)]
        op = [s.ps(f"op{k}") for k in range(2)]
        w_in, w_mm, w_copied, mask_made, wqk_ready, xb_ready, q_mm, v_mm, q_dve, q_act, v_dve, v_act = (s.sem(n) for n in (
            "w_in", "w_mm", "w_copied", "mask_made", "wqk_ready", "xb_ready", "q_mm", "v_mm", "q_dve", "q_act", "v_dve", "v_act"))
        s_mm, sim_dve, sim_act, head_done, o_dve, o_act, t_mm, x_added = (s.sem(n) for n in (
            "s_mm", "sim_dve", "sim_act", "head_done", "o_dve", "o_act", "t_mm", "x_added"))
        sums_done = s.sem("sums_done")

        def relu_count(hh, k):
            n = sum(b[4] == BLOCKS[k][4] for b in BLOCKS[:k + 1])
            return (sim_dve, hh * ND + n) if BLOCKS[k][4] else (sim_act, hh * NF + n)

        with nc.Block() as block:

            @block.sync
            def _(sp):
                for dst, src in ((wq, Wq), (wk, Wk), (wv, Wv)):
                    sp.dma_start(dst[:], src.rearrange("h e d -> e h d")).then_inc(w_in, 16)

            @block.gpsimd
            def _(pool):
                nc.gpsimd.memset(zeros[:], 0.0).then_inc(mask_made, 1)
                nc.gpsimd.memset(mask[:], 1.0 / SEQ).then_inc(mask_made, 1)
                pool.wait_ge(mask_made, 2)
                nc.gpsimd.affine_select(out=mask[:], in_=mask[:], compare_op=ALU.is_ge, fill=0.0, base=0,
                                        pattern=[[1, GROUP]], channel_multiplier=-1).then_inc(mask_made, 1)
                pool.wait_ge(w_copied, 4)
                with pool.Fori(0, BATCH) as b:
                    pool.wait_ge(head_done, b * H + 2)
                    nc.gpsimd.tensor_copy(xb[:], XT[:, bass.ds(b * SEQ, SEQ)]).then_inc(xb_ready, 1)
                    with pool.Fori(0, H // 2) as h2:
                        for par in range(2):
                            hh = b * H + h2 * 2 + par
                            pool.wait_ge(head_done, hh + 1)
                            nc.gpsimd.tensor_copy(wqk_f[:, par:par + 1], wqk[:, bass.ds(h2 * 2 + par, 1)]).then_inc(wqk_ready, 1)

            @block.tensor
            def _(pe):
                pe.wait_ge(w_in, 48)
                for h in range(H):
                    nc.tensor.matmul(sc[h // 4][:, (h % 4) * C:(h % 4 + 1) * C], wq[:, h], wk[:, h], start=True, stop=True)
                    last = nc.tensor.transpose(sc[2 + h // 4][:, (h % 4) * C:(h % 4 + 1) * C], wv[:, h], ident[:])
                last.then_inc(w_mm, 1)
                pe.wait_ge(w_copied, 4)
                pe.sem_inc(head_done, 2)
                with pe.Fori(0, BATCH) as b:
                    pe.wait_ge(mask_made, 3)
                    pe.wait_ge(x_added, b * 2 + 1)
                    pe.wait_ge(xb_ready, b + 1)
                    for half in range(2):
                        nc.tensor.matmul(op[half][:], ident[:], XT[:, bass.ds(b * SEQ + half * GROUP, GROUP)], start=True, stop=False)
                    with pe.Fori(0, H // 2) as h2:
                        for par in range(2):
                            h = h2 * 2 + par
                            hh = b * H + h
                            pe.wait_ge(wqk_ready, hh + 1)
                            for half in range(2):
                                nc.tensor.matmul(qp[half][:], wqk_f[:, par], XT[:, bass.ds(b * SEQ + half * GROUP, GROUP)],
                                                 start=True, stop=True).then_inc(q_mm, 1)
                            for m in range(KT):
                                ins = nc.tensor.matmul(sc[2 + m // TPG][:, (m % TPG) * C:(m % TPG + 1) * C], xb[:, m * P:(m + 1) * P],
                                                       wvT[:, bass.ds(h, 1), :].rearrange("p a c -> p (a c)"), start=True, stop=True)
                                if m % TPG == TPG - 1:
                                    ins.then_inc(v_mm, 1)
                            pe.wait_ge(q_dve, hh + 1)
                            pe.wait_ge(q_act, hh + 1)

                            def score(k):
                                _, m, n0, w, _ = BLOCKS[k]
                                nc.tensor.matmul(sc[k % SC][:, 0:w], xb[:, m * P:(m + 1) * P], q[:, par, n0:n0 + w],
                                                 start=True, stop=True).then_inc(s_mm, 1)

                            for k in range(SC):
                                if k == 2:
                                    pe.wait_ge(v_dve, hh + 1)
                                if k == 3:
                                    pe.wait_ge(v_act, hh + 1)
                                score(k)
                            for k, (half, m, n0, w, _) in enumerate(BLOCKS):
                                pe.wait_ge(*relu_count(hh, k))
                                ins = nc.tensor.matmul(op[half][:, n0 - half * GROUP:n0 - half * GROUP + w], v[:, par, m], sim[:, par, k, 0:w],
                                                       start=False, stop=False)
                                if k == NB - 1:
                                    ins.then_inc(head_done, 1)
                                if k + SC < NB:
                                    score(k + SC)
                    for half in range(2):
                        ins = nc.tensor.matmul(op[half][:], zeros[:, 0:P], zeros[:], start=False, stop=True)
                    ins.then_inc(sums_done, 1)
                    pe.wait_ge(o_dve, b + 1)
                    pe.wait_ge(o_act, b + 1)
                    for t in range(KT):
                        ins = nc.tensor.transpose(sc[t // TPG][:, (t % TPG) * P:(t % TPG + 1) * P], o[:, t * P:(t + 1) * P], ident[:])
                        if t % TPG == TPG - 1:
                            ins.then_inc(t_mm, 1)

            @block.scalar
            def _(act):
                act.wait_ge(w_mm, 1)
                nc.scalar.activation(wvT[:, 0:4].rearrange("p h c -> p (h c)"), sc[2][:], ACT.Copy).then_inc(w_copied, 1)
                nc.scalar.activation(wvT[:, 4:8].rearrange("p h c -> p (h c)"), sc[3][:], ACT.Copy).then_inc(w_copied, 1)
                with act.Fori(0, BATCH) as b:
                    with act.Fori(0, H // 2) as h2:
                        for par in range(2):
                            hh = b * H + h2 * 2 + par
                            act.wait_ge(head_done, hh + 1)
                            act.wait_ge(q_mm, hh * 2 + 2)
                            nc.scalar.activation(q[:, par, GROUP:], qp[1][:], ACT.Copy).then_inc(q_act, 1)
                            act.wait_ge(v_mm, hh * 2 + 2)
                            nc.scalar.activation(v[:, par, TPG:].rearrange("p k c -> p (k c)"), sc[3][:], ACT.Copy).then_inc(v_act, 1)
                            for k, blk in enumerate(BLOCKS):
                                if not blk[4]:
                                    act.wait_ge(s_mm, hh * NB + (k + 1))
                                    nc.scalar.activation(sim[:, par, k], sc[k % SC][:], ACT.Relu, scale=1.0 / SEQ).then_inc(sim_act, 1)
                    act.wait_ge(sums_done, b + 1)
                    nc.scalar.activation(o[:, GROUP:], op[1][:], ACT.Copy).then_inc(o_act, 1)

            @block.vector
            def _(dve):
                dve.wait_ge(w_mm, 1)
                nc.vector.tensor_copy(wqk[:, 0:4].rearrange("p h c -> p (h c)"), sc[0][:]).then_inc(w_copied, 1)
                nc.vector.tensor_copy(wqk[:, 4:8].rearrange("p h c -> p (h c)"), sc[1][:]).then_inc(w_copied, 1)
                dve.wait_ge(mask_made, 3)
                dve.sem_inc(x_added, 1)
                with dve.Fori(0, BATCH) as b:
                    with dve.Fori(0, H // 2) as h2:
                        for par in range(2):
                            hh = b * H + h2 * 2 + par
                            dve.wait_ge(head_done, hh + 1)
                            dve.wait_ge(q_mm, hh * 2 + 1)
                            nc.vector.tensor_copy(q[:, par, 0:GROUP], qp[0][:]).then_inc(q_dve, 1)
                            dve.wait_ge(v_mm, hh * 2 + 1)
                            nc.vector.tensor_copy(v[:, par, 0:TPG].rearrange("p k c -> p (k c)"), sc[2][:]).then_inc(v_dve, 1)
                            for k, (_, _, _, w, on_diag) in enumerate(BLOCKS):
                                if on_diag:
                                    dve.wait_ge(s_mm, hh * NB + (k + 1))
                                    nc.vector.scalar_tensor_tensor(sim[:, par, k, 0:w], sc[k % SC][:, 0:w], 0.0, mask[:, 0:w],
                                                                   ALU.max, ALU.mult).then_inc(sim_dve, 1)
                    dve.wait_ge(sums_done, b + 1)
                    nc.vector.tensor_copy(o[:, 0:GROUP], op[0][:]).then_inc(o_dve, 1)
                    for half in range(2):
                        dve.wait_ge(t_mm, b * 2 + (half + 1))
                        xt = X[:, bass.ds(b * KT + half * TPG, TPG), :]
                        nc.vector.tensor_tensor(xt, sc[half][:].rearrange("p (t c) -> p t c", c=C), xt, ALU.add).then_inc(x_added, 1)
                dve.wait_ge(x_added, 2 * BATCH + 1)
def moe_grouped(nc, X, XN, XT, ident, router_w, bias, up_w, down_w, shared_up, shared_down):
    E, I = router_w.shape[0], up_w.shape[2]
    G, TOPG, K = 8, 4, 8
    EG = E // G
    EPT = P // I
    NR = E // EPT
    NSH = shared_up.shape[1] // P
    NJ = NR + NSH
    BIG = 1e30
    HB = 4
    LAG = 2
    with Stage(nc, "grp") as s:
        rw = s.sb("rw", [E, C])
        rwT = s.sb("rwT", [P, E])
        bs = s.sb("bs", [P, E])
        up = s.sb("up", [P, E, I])
        down = s.sb("down", [P, NR, C])
        sup = s.sb("sup", [P, NSH * P])
        sdown = s.sb("sdown", [P, NSH, C])
        sg, sfc, eq, v2, gt = (s.sb(n, [P, NT, E]) for n in ("sg", "sfc", "eq", "v2", "gt"))
        reset = s.sb("reset", [P, NT, E])
        m1, m2, cnt, rank, tmp = (s.sb(n, [P, NT, G]) for n in ("m1", "m2", "cnt", "rank", "tmp"))
        top = s.sb("top", [P, NT, K])
        one = s.sb("one", [P, NT, 1])
        parts = s.sb("parts", [P, NT, 2, E], BF16)
        low = s.sb("low", [P, NT, E], BF16)
        cT2 = s.sb("cT2", [2 * E, T], BF16)
        cT1 = s.sb("cT1", [E, T], BF16)
        sel = s.sb("sel", [2 * E, NR, EPT, I], BF16)
        ident16 = s.sb("ident16", [P, P], BF16)
        r = s.sb("r", [P, 2, GROUP])
        t_ = s.sb("t", [P, 2, GROUP])
        h = s.sb("h", [P, HB, GROUP])
        oT = s.sb("oT", [P, 2, GROUP])
        ph, cb, po, tr = ([s.ps(f"{n}{k}") for k in range(2)] for n in ("ph", "cb", "po", "tr"))
        lgb = ph + cb
        rw_in, bias_in, w_in, made, rwT_mm, rwT_ready, logits_mm, sg_ready, c_ready, ct_mm, ct_ready = (s.sem(n) for n in (
            "rw_in", "bias_in", "w_in", "made", "rwT_mm", "rwT_ready", "logits_mm", "sg_ready", "c_ready", "ct_mm", "ct_ready"))
        up_mm, bc_mm, relu_done, h_done, down_mm, o_mm, o_copied, tr_mm, x_added, ch, tch = (s.sem(n) for n in (
            "up_mm", "bc_mm", "relu_done", "h_done", "down_mm", "o_mm", "o_copied", "tr_mm", "x_added", "vector_chain", "t_done"))
        low_ready = s.sem("low_ready")
        with nc.Block() as block:

            @block.sync
            def _(sp):
                sp.dma_start(rw[:], router_w).then_inc(rw_in, 16)
                sp.dma_start(bs[:], bias.rearrange("(a e) -> a e", a=1).to_broadcast([P, E])).then_inc(bias_in, 16)
                sp.dma_start(up[:], up_w.rearrange("e c i -> c e i")).then_inc(w_in, 16)
                sp.dma_start(down[:], down_w.rearrange("(j a) i c -> (a i) j c", a=EPT)).then_inc(w_in, 16)
                sp.dma_start(sup[:], shared_up).then_inc(w_in, 16)
                sp.dma_start(sdown[:], shared_down.rearrange("(k p) c -> p k c", p=P)).then_inc(w_in, 16)

            @block.gpsimd
            def _(pool):
                nc.gpsimd.memset(sel[:], 0.0).then_inc(made, 1)
                nc.gpsimd.memset(reset[:], 1.0).then_inc(made, 1)
                pool.wait_ge(made, 2)
                for n in range(2):
                    nc.gpsimd.affine_select(out=sel[:], in_=sel[:], compare_op=ALU.not_equal, fill=1.0, base=-n * E,
                                            pattern=[[-EPT, NR], [-1, EPT], [0, I]], channel_multiplier=1).then_inc(made, 1)
                    pool.wait_ge(made, 3 + n)
                nc.gpsimd.tensor_copy(ident16[:], ident[:]).then_inc(made, 1)
                nc.gpsimd.memset(reset[:, :, 0:1], 0.0).then_inc(made, 1)

            @block.tensor
            def _(pe):
                pe.wait_ge(rw_in, 16)
                nc.tensor.transpose(tr[0][:, 0:E], rw[:], ident[0:E, 0:E]).then_inc(rwT_mm, 1)
                pe.wait_ge(rwT_ready, 1)
                for i in range(NT):
                    b, k = divmod(i, NT // 4)
                    last = nc.tensor.matmul(lgb[b][:, k * E:(k + 1) * E], XT[:, i * P:(i + 1) * P], rwT[:], start=True, stop=True)
                last.then_inc(logits_mm, 1)
                pe.wait_ge(c_ready, 1)
                pe.wait_ge(made, 6)
                for i in range(NT):
                    g, k = divmod(i, TPG)
                    if k == 0 and g >= 2:
                        pe.wait_ge(ct_ready, g - 1)
                        pe.wait_ge(low_ready, g - 1)
                    nc.tensor.transpose(tr[g % 2][:].bitcast(BF16)[:, k * P:(k + 1) * P],
                                        parts[:, i].rearrange("p n e -> p (n e)"), ident16[:]).then_inc(ct_mm, 1)
                    nc.tensor.transpose(po[g % 2][:].bitcast(BF16)[0:E, k * P:(k + 1) * P], low[:, i], ident16[:]).then_inc(ct_mm, 1)
                pe.wait_ge(w_in, 64)
                pe.wait_ge(made, 6)
                pe.wait_ge(ct_ready, NG)
                pe.wait_ge(low_ready, NG)
                with pe.Fori(0, NG // 2) as g2:
                    for par in range(2):
                        g = g2 * 2 + par

                        def down_product(j):
                            J = g * NJ + j
                            pe.wait_ge(h_done, J + 3)
                            w = down[:, j] if j < NR else sdown[:, j - NR]
                            ins = nc.tensor.matmul(po[par][:], w, h[:, (par * NJ + j) % HB], start=(j == 0), stop=(j == NJ - 1))
                            ins.then_inc(down_mm, 1)

                        for j in range(NJ):
                            J = g * NJ + j
                            pe.wait_ge(relu_done, J + 1)
                            w = up[:, EPT * j:EPT * (j + 1)].rearrange("p a i -> p (a i)") if j < NR else sup[:, (j - NR) * P:(j - NR + 1) * P]
                            nc.tensor.matmul(ph[j % 2][:], w, XT[:, bass.ds(g * GROUP, GROUP)], start=True, stop=True).then_inc(up_mm, 1)
                            if j < NR:
                                pe.wait_ge(h_done, J + 1)
                                pick = sel[:, j].rearrange("k a i -> k (a i)")
                                nc.tensor.matmul(cb[j % 2][:], pick, cT2[:, bass.ds(g * GROUP, GROUP)], start=True, stop=False)
                                nc.tensor.matmul(cb[j % 2][:], pick[0:E], cT1[:, bass.ds(g * GROUP, GROUP)],
                                                 start=False, stop=True).then_inc(bc_mm, 1)
                            if j >= LAG:
                                down_product(j - LAG)
                        for j in range(NJ - LAG, NJ):
                            down_product(j)
                        pe.wait_ge(o_copied, g + 1)
                        pe.wait_ge(x_added, g + 1)
                        for t in range(TPG):
                            ins = nc.tensor.transpose(tr[par][:, t * P:(t + 1) * P], oT[:, par, t * P:(t + 1) * P], ident[:])
                        ins.then_inc(tr_mm, 1)

            @block.scalar
            def _(act):
                act.wait_ge(rwT_mm, 1)
                nc.scalar.activation(rwT[:], tr[0][:, 0:E], ACT.Copy).then_inc(rwT_ready, 1)
                act.wait_ge(logits_mm, 1)
                for b in range(4):
                    nc.scalar.activation(sg[:, b * 8:(b + 1) * 8].rearrange("p t e -> p (t e)"), lgb[b][:], ACT.Sigmoid).then_inc(sg_ready, 1)
                for g in range(NG):
                    act.wait_ge(ct_mm, 2 * TPG * (g + 1))
                    nc.scalar.activation(cT2[:, g * GROUP:(g + 1) * GROUP], tr[g % 2][:].bitcast(BF16)[:, 0:GROUP], ACT.Copy).then_inc(ct_ready, 1)
                act.wait_ge(ct_ready, NG)
                act.sem_inc(relu_done, 2)
                with act.Fori(0, NG // 2) as g2:
                    for par in range(2):
                        g = g2 * 2 + par
                        for j in range(NJ):
                            J = g * NJ + j
                            act.wait_ge(h_done, J + 1)
                            act.wait_ge(up_mm, J + 1)
                            nc.scalar.activation(r[:, j % 2], ph[j % 2][:], ACT.Relu).then_inc(relu_done, 1)
                        act.wait_ge(down_mm, g * NJ + (NJ + HB))
                        act.wait_ge(x_added, g + 1)
                        nc.scalar.activation(oT[:, par], po[par][:], ACT.Copy).then_inc(o_copied, 1)

            @block.vector
            def _(dve):
                c = Chain(dve, ch)
                dve.wait_ge(bias_in, 16)
                dve.wait_ge(sg_ready, 4)
                tt, ts, stt, red = nc.vector.tensor_tensor, nc.vector.tensor_scalar, nc.vector.scalar_tensor_tensor, nc.vector.tensor_reduce

                def grp(a):
                    return a[:].rearrange("p t (g e) -> p (t g) e", e=EG)

                def flat(a):
                    return a[:].rearrange("p t g -> p (t g)")

                NGR = NT * G
                c.link(tt(sfc[:], sg[:], bs[:].unsqueeze(1).to_broadcast([P, NT, E]), ALU.add))
                c.link(red(flat(m1), grp(sfc), AX.X, ALU.max))
                c.link(tt(grp(eq), grp(sfc), bcast(flat(m1), EG), ALU.is_equal))
                c.link(red(flat(cnt), grp(eq), AX.X, ALU.add))
                c.link(stt(flat(v2), flat(eq), -BIG, flat(sfc), ALU.mult, ALU.add))
                c.link(red(flat(m2), grp(v2), AX.X, ALU.max))
                c.link(ts(cnt[:], cnt[:], 1.5, -BIG, ALU.is_lt, ALU.mult))
                c.link(tt(cnt[:], cnt[:], m1[:], ALU.add))
                c.link(tt(m2[:], m2[:], cnt[:], ALU.max))
                c.link(tt(m1[:], m1[:], m2[:], ALU.add))
                descending_rank(nc, c, rank, tmp, m1, G)
                c.link(ts(rank[:], rank[:], TOPG - 0.5, None, ALU.is_lt))
                c.link(tt(grp(v2), grp(sfc), bcast(flat(rank), EG), ALU.mult))
                for i in range(NT):
                    nc.vector.max(top[:, i], v2[:, i]).then_inc(ch, 1)
                c.n += NT
                dve.wait_ge(ch, c.n)
                thr = top[:, :, K - 1:K].to_broadcast([P, NT, E])
                c.link(tt(gt[:], v2[:], thr, ALU.is_gt))
                c.link(tt(eq[:], v2[:], thr, ALU.is_equal))
                c.link(red(one[:], gt[:], AX.X, ALU.add))
                dve.wait_ge(made, 6)
                c.link(nc.vector.tensor_tensor_scan(flat(v2), flat(reset), flat(eq), 0.0, ALU.mult, ALU.add))
                c.link(tt(v2[:], v2[:], one[:].to_broadcast([P, NT, E]), ALU.add))
                c.link(stt(flat(v2), flat(v2), K + 0.5, flat(eq), ALU.is_lt, ALU.mult))
                c.link(tt(gt[:], gt[:], v2[:], ALU.add))
                c.link(tt(gt[:], gt[:], sg[:], ALU.mult))
                c.link(red(one[:], gt[:], AX.X, ALU.add))
                c.link(ts(one[:], one[:], 1e-20, None, ALU.add))
                c.link(nc.vector.reciprocal(one[:], one[:]))
                c.link(tt(gt[:], gt[:], one[:].to_broadcast([P, NT, E]), ALU.mult))
                c.link(ts(gt[:], gt[:], 2.5, None, ALU.mult))
                c.link(nc.vector.tensor_copy(parts[:, :, 0], gt[:]))
                c.link(tt(gt[:], gt[:], parts[:, :, 0], ALU.subtract))
                c.link(nc.vector.tensor_copy(parts[:, :, 1], gt[:]))
                tt(low[:], gt[:], parts[:, :, 1], ALU.subtract).then_inc(c_ready, 1)
                for g in range(NG):
                    dve.wait_ge(ct_mm, 2 * TPG * (g + 1))
                    nc.vector.tensor_copy(cT1[:, g * GROUP:(g + 1) * GROUP], po[g % 2][:].bitcast(BF16)[0:E, 0:GROUP]).then_inc(low_ready, 1)
                dve.wait_ge(ct_ready, NG)
                dve.sem_inc(h_done, 2)
                dve.sem_inc(down_mm, HB)
                dve.sem_inc(x_added, 1)
                with dve.Fori(0, NG // 2) as g2:
                    for par in range(2):
                        g = g2 * 2 + par
                        for j in range(NJ):
                            J = g * NJ + j
                            dve.wait_ge(relu_done, J + 3)
                            if j < NR:
                                dve.wait_ge(bc_mm, g * NR + (j + 1))
                                tt(t_[:, j % 2], r[:, j % 2], cb[j % 2][:], ALU.mult).then_inc(tch, 1)
                                dve.wait_ge(tch, g * NR + (j + 1))
                            dve.wait_ge(down_mm, J + 1)
                            a = t_ if j < NR else r
                            tt(h[:, (par * NJ + j) % HB], a[:, j % 2], r[:, j % 2], ALU.mult).then_inc(h_done, 1)
                        dve.wait_ge(tr_mm, g + 1)
                        xt = X[:, bass.ds(g * TPG, TPG), :]
                        tt(xt, tr[par][:].rearrange("p (t c) -> p t c", c=C), xt, ALU.add).then_inc(x_added, 1)
                dve.wait_ge(x_added, NG + 1)
def selective_scan(nc, X, XN, XT, ident, in_proj_w, conv_w, conv_b, x_proj_w, A_log, D, out_proj_w):
    DI, TAPS = conv_w.shape[0], conv_w.shape[2]
    CT = DI // P
    N = A_log.shape[0]
    PAD = TAPS - 1
    with Stage(nc, "ssm") as s:
        xc, z = (s.sb(n, [P, CT, T]) for n in ("xc", "z"))
        delta = s.sb("delta", [P, T])
        bc = s.sb("bc", [3 * 2 * N, T], BF16)
        negA = s.sb("negA", [P, N])
        Ds = s.sb("Ds", [P, CT])
        woT = s.sb("woT", [P, CT, C])
        sel = s.sb("sel", [3 * 2 * N, 2 * N, P], BF16)
        with Stage(nc, "proj") as s1:
            wi = s1.sb("wi", [P, 2 * CT, C])
            wiT = s1.sb("wiT", [P, 2 * CT * P])
            wx = s1.sb("wx", [1 + 2 * N, DI])
            wxT = s1.sb("wxT", [P, CT, 1 + 2 * N])
            wx3 = s1.sb("wx3", [P, CT, 3, 2 * N])
            wo = s1.sb("wo", [P, DI])
            cw = s1.sb("cw", [P, CT, TAPS])
            cbias = s1.sb("cbias", [P, CT])
            xin = s1.sb("xin", [P, 2, CT, PAD + SEQ])
            t1 = s1.sb("t1", [3 * 2 * N, GROUP], BF16)
            r1 = s1.sb("r1", [3 * 2 * N, GROUP])
            t2 = s1.sb("t2", [3 * 2 * N, GROUP], BF16)
            e1 = s1.sb("e1", [P, GROUP])
            e2 = s1.sb("e2", [P, GROUP])
            pj = [s1.ps(f"pj{k}") for k in range(4)]
            pd = [s1.ps(f"pd{k}") for k in range(2)]
            px = [s1.ps(f"px{k}") for k in range(2)]
            w_in, c_in, w_mm, w_copied, wx_ready, padded, pj_mm, x_copied, z_ready, conv_ready, xc_ready = (s1.sem(n) for n in (
                "w_in", "c_in", "w_mm", "w_copied", "wx_ready", "padded", "pj_mm", "x_copied", "z_ready", "conv_ready", "xc_ready"))
            pd_mm, px_mm, delta_ready, bc_ready, ch, ach, made = (s1.sem(n) for n in (
                "pd_mm", "px_mm", "delta_ready", "bc_ready", "vector_chain", "scalar_chain", "made"))
            apart = s.sem("apart")
            with nc.Block() as block:

                @block.sync
                def _(sp):
                    sp.dma_start(wi[:], in_proj_w.rearrange("(k p) c -> p k c", p=P)).then_inc(w_in, 16)
                    sp.dma_start(wx[:], x_proj_w).then_inc(w_in, 16)
                    sp.dma_start(wo[:], out_proj_w).then_inc(w_in, 16)
                    sp.dma_start(cw[:], conv_w.rearrange("(k p) a t -> p k (a t)", p=P)).then_inc(c_in, 16)
                    sp.dma_start(cbias[:], conv_b.rearrange("(k p) -> p k", p=P)).then_inc(c_in, 16)
                    sp.dma_start(Ds[:], D.rearrange("(k p) -> p k", p=P)).then_inc(c_in, 16)
                    sp.dma_start(negA[:], A_log.rearrange("(a n) -> a n", a=1).to_broadcast([P, N])).then_inc(c_in, 16)

                @block.gpsimd
                def _(pool):
                    nc.gpsimd.memset(sel[:], 0.0).then_inc(made, 1)
                    nc.gpsimd.memset(xin[:, :, :, 0:PAD], 0.0).then_inc(padded, 1)
                    for n in range(3):
                        pool.wait_ge(made, n + 1)
                        nc.gpsimd.affine_select(out=sel[:], in_=sel[:], compare_op=ALU.not_equal, fill=1.0, base=-n * 2 * N,
                                                pattern=[[-1, 2 * N], [0, P]], channel_multiplier=1).then_inc(made, 1)
                    pool.wait_ge(made, 4)

                @block.tensor
                def _(pe):
                    pe.wait_ge(w_in, 48)
                    for k in range(2 * CT):
                        nc.tensor.transpose(pj[0][:, k * P:(k + 1) * P], wi[:, k], ident[:])
                    for k in range(CT):
                        nc.tensor.transpose(pj[1][:, k * P:(k + 1) * P], wo[:, k * P:(k + 1) * P], ident[:])
                        last = nc.tensor.transpose(pj[2][:, k * P:k * P + 1 + 2 * N], wx[:, k * P:(k + 1) * P], ident[0:1 + 2 * N, 0:1 + 2 * N])
                    last.then_inc(w_mm, 1)
                    pe.wait_ge(w_copied, 3)
                    pe.wait_ge(wx_ready, 1)
                    with pe.Fori(0, BATCH) as b:
                        for k in range(2 * CT):
                            for half in range(2):
                                n = k * 2 + half
                                if k < CT:
                                    pe.wait_ge(z_ready, b * 4 + (n + 1))
                                else:
                                    pe.wait_ge(x_copied, b * 4 + (n - 3))
                                nc.tensor.matmul(pj[n % 4][:], wiT[:, k * P:(k + 1) * P], XT[:, bass.ds(b * SEQ + half * GROUP, GROUP)],
                                                 start=True, stop=True).then_inc(pj_mm, 1)
                        pe.wait_ge(xc_ready, (b + 1) * CT)
                        for half in range(2):
                            src = [xc[:, k, bass.ds(b * SEQ + half * GROUP, GROUP)] for k in range(CT)]
                            pe.wait_ge(delta_ready, b * 2 + (half + 1))
                            for k in range(CT):
                                ins = nc.tensor.matmul(pd[half][:], wxT[:, k, 0:1].to_broadcast([P, P]), src[k], start=(k == 0), stop=(k == CT - 1))
                            ins.then_inc(pd_mm, 1)
                            pe.wait_ge(bc_ready, b * 2 + (half + 1))
                            for k in range(CT):
                                ins = nc.tensor.matmul(px[half][0:6 * N, :], wx3[:, k].rearrange("p a n -> p (a n)"), src[k], start=(k == 0), stop=(k == CT - 1))
                            ins.then_inc(px_mm, 1)

                @block.scalar
                def _(act):
                    act.wait_ge(c_in, 64)
                    nc.scalar.activation(negA[:], negA[:], ACT.Exp).then_inc(ach, 1)
                    act.wait_ge(w_mm, 1)
                    nc.scalar.activation(wiT[:], pj[0][:], ACT.Copy).then_inc(w_copied, 1)
                    nc.scalar.activation(woT[:].rearrange("p k c -> p (k c)"), pj[1][:, 0:CT * P], ACT.Copy).then_inc(w_copied, 1)
                    nc.scalar.activation(wxT[:], pj[2][:, 0:CT * P].rearrange("p (k c) -> p k c", c=P)[:, :, 0:1 + 2 * N], ACT.Copy).then_inc(w_copied, 1)
                    act.sem_inc(z_ready, 4)
                    act.sem_inc(delta_ready, 2)
                    act.wait_ge(padded, 1)
                    with act.Fori(0, BATCH // 2) as b2:
                        for par in range(2):
                            b = b2 * 2 + par
                            for n in range(8):
                                k, half = divmod(n, 2)
                                act.wait_ge(pj_mm, b * 8 + (n + 1))
                                if k < CT:
                                    act.wait_ge(conv_ready, (b + 1) * CT)
                                    nc.scalar.activation(xin[:, par, k, PAD + half * GROUP:PAD + (half + 1) * GROUP], pj[n % 4][:], ACT.Copy).then_inc(x_copied, 1)
                                else:
                                    act.sem_inc(apart, 1)
                                    nc.scalar.activation(z[:, k - CT, bass.ds(b * SEQ + half * GROUP, GROUP)], pj[n % 4][:], ACT.Silu).then_inc(z_ready, 1)
                            for k in range(CT):
                                act.wait_ge(conv_ready, b * CT + (k + 1 + 2 * CT))
                                xs = xc[:, k, bass.ds(b * SEQ, SEQ)]
                                act.sem_inc(apart, 1)
                                nc.scalar.activation(xs, xs, ACT.Silu, bias=cbias[:, k:k + 1]).then_inc(xc_ready, 1)
                            for half in range(2):
                                act.wait_ge(pd_mm, b * 2 + (half + 1))
                                act.wait_ge(delta_ready, b * 2 + (half + 2))
                                nc.scalar.activation(e1[:], pd[half][:], ACT.Abs).then_inc(ach, 1)
                                act.wait_ge(ach, (b * 2 + half) * 3 + 2)
                                nc.scalar.activation(e1[:], e1[:], ACT.Exp, scale=-1.0).then_inc(ach, 1)
                                act.wait_ge(ach, (b * 2 + half) * 3 + 3)
                                nc.scalar.activation(e1[:], e1[:], ACT.Ln, bias=1.0).then_inc(ach, 1)

                @block.vector
                def _(dve):
                    c = Chain(dve, ch)
                    tt, ts, stt = nc.vector.tensor_tensor, nc.vector.tensor_scalar, nc.vector.scalar_tensor_tensor
                    dve.wait_ge(w_copied, 3)
                    nc.vector.tensor_copy(wx3[:], wxT[:, :, 1:].unsqueeze(2).to_broadcast([P, CT, 3, 2 * N])).then_inc(wx_ready, 1)
                    dve.wait_ge(ach, 1)
                    c.link(ts(negA[:], negA[:], -1.0, None, ALU.mult))
                    dve.sem_inc(conv_ready, 2 * CT)
                    dve.sem_inc(bc_ready, 2)
                    base = c.n
                    LINKS = (TAPS - 1) * CT + 2 * 4
                    with dve.Fori(0, BATCH // 2) as b2:
                        for par in range(2):
                            b = b2 * 2 + par
                            cc = Chain(dve, ch, base + b * LINKS)
                            for k in range(CT):
                                dve.wait_ge(x_copied, b * 4 + (2 * k + 2))
                                xs = xc[:, k, bass.ds(b * SEQ, SEQ)]
                                cc.link(ts(xs, xin[:, par, k, 0:SEQ], cw[:, k, 0:1], None, ALU.mult))
                                for j in range(1, TAPS):
                                    ins = stt(xs, xin[:, par, k, j:j + SEQ], cw[:, k, j:j + 1], xs, ALU.mult, ALU.add)
                                    if j < TAPS - 1:
                                        cc.link(ins)
                                    else:
                                        ins.then_inc(conv_ready, 1)
                            for half in range(2):
                                at = bass.ds(b * SEQ + half * GROUP, GROUP)
                                dve.wait_ge(ach, (b * 2 + half) * 3 + 4)
                                stt(delta[:, at], pd[half][:], 0.0, e1[:], ALU.max, ALU.add).then_inc(delta_ready, 1)
                                dve.wait_ge(px_mm, b * 2 + (half + 1))
                                v = px[half][0:6 * N, :]
                                cc.link(nc.vector.tensor_copy(t1[:], v))
                                nc.vector.tensor_copy(bc[0:2 * N, at], t1[0:2 * N])
                                cc.link(tt(r1[:], v, t1[:], ALU.subtract))
                                cc.link(nc.vector.tensor_copy(t2[:], r1[:]))
                                nc.vector.tensor_copy(bc[2 * N:4 * N, at], t2[2 * N:4 * N])
                                ins = tt(bc[4 * N:6 * N, at], r1[4 * N:6 * N], t2[4 * N:6 * N], ALU.subtract)
                                cc.link(ins)
                                dve.sem_inc(bc_ready, 1)
                            assert cc.n == LINKS, cc.n
                    dve.wait_ge(delta_ready, 2 * BATCH + 2)

        xdt = s.sb("xdt", [P, CT, SEQ])
        dA = s.sb("dA", [P, 2, SEQ])
        u = s.sb("u", [P, 2, SEQ])
        h = s.sb("h", [P, 2, CT, SEQ])
        hc = XN[:].rearrange("p (a k t) c -> p a k (t c)", a=2, k=CT)
        cs = s.sb("cs", [P, 2, SEQ])
        cs_ready = s.sem("cs_ready")
        pB, pC = ([s.ps(f"{n}{k}") for k in range(2)] for n in ("pB", "pC"))
        py = [s.ps(f"py{k}") for k in range(4)]
        b_mm, c_mm, dA_ready, u_ready, scanned, hc_ready, sum_mm, y_ready, out_mm, x_added, ch = (s.sem(n) for n in (
            "b_mm", "c_mm", "dA_ready", "u_ready", "scanned", "hc_ready", "sum_mm", "y_ready", "out_mm", "x_added", "vector_chain2"))
        yt = s.sb("yt", [P, CT, SEQ])
        with nc.Block() as block:

            @block.tensor
            def _(pe):
                pe.sem_inc(sum_mm, 2 * CT)
                with pe.Fori(0, BATCH) as b:
                    pe.wait_ge(x_added, b * 2 + 1)

                    def accumulate(n, ct):
                        U = b * (N * CT) + (n * CT + ct)
                        pe.wait_ge(hc_ready, U + (1 + 2 * CT))
                        for half in range(2):
                            ins = nc.tensor.matmul(py[ct * 2 + half][:], ident[:], hc[:, n % 2, ct, half * GROUP:(half + 1) * GROUP],
                                                   start=(n == 0), stop=(n == N - 1))
                        ins.then_inc(sum_mm, 1)

                    for n in range(N):
                        U = b * (N * CT) + n * CT
                        pe.wait_ge(u_ready, U + 1)
                        for half in range(2):
                            ins = nc.tensor.matmul(pB[half][:], sel[:, n], bc[:, bass.ds(b * SEQ + half * GROUP, GROUP)], start=True, stop=True)
                        ins.then_inc(b_mm, 1)
                        pe.wait_ge(cs_ready, b * N + (n + 1))
                        for half in range(2):
                            ins = nc.tensor.matmul(pC[half][:], sel[:, N + n], bc[:, bass.ds(b * SEQ + half * GROUP, GROUP)], start=True, stop=True)
                        ins.then_inc(c_mm, 1)
                        if n:
                            accumulate(n - 1, 0)
                            accumulate(n - 1, 1)
                    accumulate(N - 1, 0)
                    accumulate(N - 1, 1)
                    pe.wait_ge(y_ready, b + 1)
                    for t in range(SEQ // P):
                        o = pB[t // TPG][:, (t % TPG) * C:(t % TPG + 1) * C]
                        for k in range(CT):
                            ins = nc.tensor.matmul(o, yt[:, k, t * P:(t + 1) * P], woT[:, k], start=(k == 0), stop=(k == CT - 1))
                    ins.then_inc(out_mm, 1)

            @block.gpsimd
            def _(pool):
                with pool.Fori(0, BATCH) as b:
                    for n in range(N):
                        pool.wait_ge(cs_ready, b * N + (n + 2))
                        for k in range(CT):
                            U = b * (N * CT) + (n * CT + k)
                            pool.wait_ge(scanned, U + (1 + 2 * CT))
                            pool.wait_ge(sum_mm, U + 1)
                            nc.gpsimd.tensor_tensor(hc[:, n % 2, k], cs[:, n % 2], h[:, n % 2, k], ALU.mult).then_inc(hc_ready, 1)

            @block.scalar
            def _(act):
                act.sem_inc(scanned, 2 * CT)
                act.sem_inc(cs_ready, 1)
                with act.Fori(0, BATCH) as b:
                    for n in range(N):
                        act.wait_ge(scanned, b * (N * CT) + (n * CT + CT))
                        act.sem_inc(apart, 1)
                        nc.scalar.activation(dA[:, n % 2], delta[:, bass.ds(b * SEQ, SEQ)], ACT.Exp, scale=negA[:, n:n + 1]).then_inc(dA_ready, 1)
                        act.wait_ge(c_mm, b * N + (n + 1))
                        act.wait_ge(hc_ready, b * (N * CT) + (n * CT + 1))
                        for half in range(2):
                            ins = nc.scalar.activation(cs[:, n % 2, half * GROUP:(half + 1) * GROUP], pC[half][:], ACT.Copy)
                        ins.then_inc(cs_ready, 1)

            @block.vector
            def _(dve):
                tt, ts, stt = nc.vector.tensor_tensor, nc.vector.tensor_scalar, nc.vector.scalar_tensor_tensor
                dve.sem_inc(u_ready, 1)
                dve.sem_inc(hc_ready, 2 * CT)
                dve.sem_inc(x_added, 1)
                LINKS = CT + 2 * CT - 1
                with dve.Fori(0, BATCH) as b:
                    cc = Chain(dve, ch, b * LINKS)
                    for k in range(CT):
                        cc.link(tt(xdt[:, k], xc[:, k, bass.ds(b * SEQ, SEQ)], delta[:, bass.ds(b * SEQ, SEQ)], ALU.mult))
                    for n in range(N):
                        dve.wait_ge(b_mm, b * N + (n + 1))
                        dve.wait_ge(scanned, b * (N * CT) + (n * CT + 2 * CT))
                        for k in range(CT):
                            for half in range(2):
                                ins = tt(u[:, k, half * GROUP:(half + 1) * GROUP], pB[half][:], xdt[:, k, half * GROUP:(half + 1) * GROUP], ALU.mult)
                            ins.then_inc(u_ready, 1)
                        dve.wait_ge(dA_ready, b * N + (n + 1))
                        for k in range(CT):
                            U = b * (N * CT) + (n * CT + k)
                            dve.wait_ge(u_ready, U + 2)
                            dve.wait_ge(hc_ready, U + 1)
                            nc.vector.tensor_tensor_scan(h[:, n % 2, k], dA[:, n % 2], u[:, k], 0.0, ALU.mult, ALU.add).then_inc(scanned, 1)
                    dve.wait_ge(sum_mm, (b + 1) * (N * CT) + 2 * CT)
                    for k in range(CT):
                        for half in range(2):
                            ins = stt(yt[:, k, half * GROUP:(half + 1) * GROUP], xc[:, k, bass.ds(b * SEQ + half * GROUP, GROUP)], Ds[:, k:k + 1],
                                      py[k * 2 + half][:], ALU.mult, ALU.add)
                        cc.link(ins)
                        ins = tt(yt[:, k], yt[:, k], z[:, k, bass.ds(b * SEQ, SEQ)], ALU.mult)
                        if k < CT - 1:
                            cc.link(ins)
                        else:
                            ins.then_inc(y_ready, 1)
                    dve.wait_ge(out_mm, b + 1)
                    for half in range(2):
                        xt = X[:, bass.ds(b * (SEQ // P) + half * TPG, TPG), :]
                        tt(xt, pB[half][:].rearrange("p (t c) -> p t c", c=C), xt, ALU.add).then_inc(x_added, 1)
                    assert cc.n == CT + 2 * CT - 1, cc.n
                dve.wait_ge(x_added, 2 * BATCH + 1)
def capacity_route(nc, XT, ident, router_w, FT, sel, capacity):
    E = router_w.shape[0]
    with Stage(nc, "route") as s:
        rw = s.sb("rw", [E, C])
        rwT = s.sb("rwT", [P, E])
        lg, ex, rank, tmp, hot = (s.sb(n, [P, NT, E]) for n in ("lg", "ex", "rank", "tmp", "hot"))
        hot16 = s.sb("hot16", [P, NT, E], BF16)
        red, prob, keep = (s.sb(n, [P, NT, 1]) for n in ("red", "prob", "keep"))
        pb = s.sb("pb", [P, T])
        before = s.sb("before", [P, P])
        ahead = s.sb("ahead", [P, 2, T], BF16)
        cnt = s.sb("cnt", [E, T])
        ident16 = s.sb("ident16", [P, P], BF16)
        bank = [s.ps(f"bank{k}") for k in range(8)]
        rw_in, made, rwT_mm, rwT_ready, logits_mm, shifted, exp_ready, prob_ready, pb_mm, pb_ready = (s.sem(n) for n in (
            "rw_in", "made", "rwT_mm", "rwT_ready", "logits_mm", "shifted", "exp_ready", "prob_ready", "pb_mm", "pb_ready"))
        ahead_ready, cnt_mm, cnt_ready, cntT_mm, final_ready, ft_mm, ft_ready, ch = (s.sem(n) for n in (
            "ahead_ready", "cnt_mm", "cnt_ready", "cntT_mm", "final_ready", "ft_mm", "ft_ready", "vector_chain"))
        with nc.Block() as block:

            @block.sync
            def _(sp):
                sp.dma_start(rw[:], router_w).then_inc(rw_in, 16)

            @block.gpsimd
            def _(pool):
                nc.gpsimd.memset(before[:], LEAST).then_inc(made, 1)
                nc.gpsimd.memset(sel[:], 0.0).then_inc(made, 1)
                pool.wait_ge(made, 2)
                nc.gpsimd.affine_select(out=before[:], in_=before[:], compare_op=ALU.is_gt, fill=0.0, base=0,
                                        pattern=[[1, P]], channel_multiplier=-1).then_inc(made, 1)
                nc.gpsimd.affine_select(out=sel[:], in_=sel[:], compare_op=ALU.not_equal, fill=1.0, base=0,
                                        pattern=[[-1, E], [0, P]], channel_multiplier=1).then_inc(made, 1)
                nc.gpsimd.tensor_copy(ident16[:], ident[:]).then_inc(made, 1)

            @block.tensor
            def _(pe):
                pe.wait_ge(rw_in, 16)
                nc.tensor.transpose(bank[0][:, 0:E], rw[:], ident[0:E, 0:E]).then_inc(rwT_mm, 1)
                pe.wait_ge(rwT_ready, 1)
                for i in range(NT):
                    last = nc.tensor.matmul(bank[1][:, i * E:(i + 1) * E], XT[:, i * P:(i + 1) * P], rwT[:], start=True, stop=True)
                last.then_inc(logits_mm, 1)
                pe.wait_ge(prob_ready, 1)
                for i in range(NT):
                    g, k = divmod(i, TPG)
                    if k == 0 and g >= 2:
                        pe.wait_ge(pb_ready, g - 1)
                    nc.tensor.transpose(bank[2 + g % 2][:, k * P:(k + 1) * P], prob[:, i].to_broadcast([P, P]), ident[:]).then_inc(pb_mm, 1)
                pe.wait_ge(pb_ready, NG)
                for i in range(NT):
                    pe.wait_ge(ahead_ready, i + 1)
                    for k in range(NG):
                        ins = nc.tensor.matmul(bank[k][0:E, :], hot16[:, i], ahead[:, i % 2, k * GROUP:(k + 1) * GROUP],
                                               start=(i == 0), stop=(i == NT - 1))
                    ins.then_inc(cnt_mm, 1)
                pe.wait_ge(cnt_ready, NG)
                for i in range(NT):
                    ins = nc.tensor.transpose(bank[0][:, i * E:(i + 1) * E], cnt[:, i * P:(i + 1) * P], ident[0:E, 0:E])
                ins.then_inc(cntT_mm, 1)
                pe.wait_ge(final_ready, 1)
                pe.wait_ge(made, 5)
                for i in range(NT):
                    g, k = divmod(i, TPG)
                    ins = nc.tensor.transpose(bank[g][:].bitcast(BF16)[0:E, k * P:(k + 1) * P], hot16[:, i], ident16[:])
                    if k == TPG - 1:
                        ins.then_inc(ft_mm, 1)

            @block.scalar
            def _(act):
                act.wait_ge(rwT_mm, 1)
                nc.scalar.activation(rwT[:], bank[0][:, 0:E], ACT.Copy).then_inc(rwT_ready, 1)
                act.wait_ge(shifted, 1)
                nc.scalar.activation(ex[:], lg[:], ACT.Exp).then_inc(exp_ready, 1)
                for g in range(NG):
                    act.wait_ge(pb_mm, TPG * (g + 1))
                    nc.scalar.activation(pb[:, g * GROUP:(g + 1) * GROUP], bank[2 + g % 2][:], ACT.Copy).then_inc(pb_ready, 1)
                act.wait_ge(cnt_mm, NT)
                for k in range(NG):
                    nc.scalar.activation(cnt[:, k * GROUP:(k + 1) * GROUP], bank[k][0:E, :], ACT.Copy).then_inc(cnt_ready, 1)
                for g in range(NG):
                    act.wait_ge(ft_mm, g + 1)
                    nc.scalar.activation(FT[:, g * GROUP:(g + 1) * GROUP], bank[g][:].bitcast(BF16)[0:E, 0:GROUP], ACT.Copy).then_inc(ft_ready, 1)
                act.wait_ge(ft_ready, NG)

            @block.vector
            def _(dve):
                c = Chain(dve, ch)
                tt, ts, stt, redu = nc.vector.tensor_tensor, nc.vector.tensor_scalar, nc.vector.scalar_tensor_tensor, nc.vector.tensor_reduce
                dve.wait_ge(logits_mm, 1)
                c.link(nc.vector.tensor_copy(lg[:], bank[1][:, 0:NT * E].rearrange("p (t e) -> p t e", e=E)))
                c.link(redu(red[:], lg[:], AX.X, ALU.max))
                tt(lg[:], lg[:], red[:].to_broadcast([P, NT, E]), ALU.subtract).then_inc(shifted, 1)
                dve.wait_ge(exp_ready, 1)
                c.link(redu(red[:], ex[:], AX.X, ALU.add))
                nc.vector.reciprocal(prob[:], red[:]).then_inc(prob_ready, 1)
                descending_rank(nc, c, rank, tmp, ex, E)
                c.link(ts(hot[:], rank[:], 0.5, None, ALU.is_lt))
                c.link(nc.vector.tensor_copy(hot16[:], hot[:]))
                dve.wait_ge(prob_ready, 1)
                dve.wait_ge(pb_ready, NG)
                dve.wait_ge(made, 5)
                for i in range(NT):
                    if i >= 2:
                        dve.wait_ge(cnt_mm, i - 1)
                    a, b, p_i = i * P, (i + 1) * P, prob[:, i]
                    if i:
                        ts(ahead[:, i % 2, 0:a], pb[:, 0:a], p_i, None, ALU.is_lt)
                    if i < NT - 1:
                        ts(ahead[:, i % 2, b:], pb[:, b:], p_i, None, ALU.is_le)
                    stt(ahead[:, i % 2, a:b], pb[:, a:b], p_i, before[:], ALU.subtract, ALU.is_lt).then_inc(ahead_ready, 1)
                    dve.wait_ge(ahead_ready, i + 1)
                dve.wait_ge(cntT_mm, 1)
                c.link(tt(tmp[:], hot[:], bank[0][:, 0:NT * E].rearrange("p (t e) -> p t e", e=E), ALU.mult))
                c.link(redu(red[:], tmp[:], AX.X, ALU.add))
                c.link(ts(keep[:], red[:], capacity - 0.5, None, ALU.is_lt))
                c.link(tt(hot[:], hot[:], keep[:].to_broadcast([P, NT, E]), ALU.mult))
                c.link(ts(keep[:], keep[:], -1.0, 1.0, ALU.mult, ALU.add))
                c.link(tt(hot[:, :, 0:1], hot[:, :, 0:1], keep[:], ALU.add))
                nc.vector.tensor_copy(hot16[:], hot[:]).then_inc(final_ready, 1)


def moe_capacity(nc, X, XN, XT, ident, router_w, W1, b1, W2, b2):
    E, F = W1.shape[0], W1.shape[2]
    KT = F // P
    NJ = E * KT
    HB, LAG = 4, 2
    with Stage(nc, "cap") as s:
        FT = s.sb("FT", [E, T], BF16)
        sel = s.sb("sel", [E, E, P], BF16)
        w1 = s.sb("w1", [P, E, F])
        w2 = s.sb("w2", [P, NJ, C])
        b1s = s.sb("b1", [P, NJ])
        b2s = s.sb("b2", [P, E])
        h = s.sb("h", [P, HB, GROUP])
        m = s.sb("m", [P, 2, GROUP])
        y = s.sb("y", [P, GROUP])
        acc = s.sb("acc", [P, 2, GROUP])
        w_in = s.sem("w_in")
        capacity_route(nc, XT, ident, router_w, FT, sel, -(-T * 5 // (E * 4)))
        ph, mb, po, tr = ([s.ps(f"{n}{k}") for k in range(2)] for n in ("ph", "mb", "po", "tr"))
        up_mm, relu_done, down_mm, mask_mm, mask_ready, y_done, acc_chain, acc_ready, tr_mm, x_added = (s.sem(n) for n in (
            "up_mm", "relu_done", "down_mm", "mask_mm", "mask_ready", "y_done", "acc_chain", "acc_ready", "tr_mm", "x_added"))
        with nc.Block() as block:

            @block.sync
            def _(sp):
                sp.dma_start(w1[:], W1.rearrange("e c f -> c e f")).then_inc(w_in, 16)
                sp.dma_start(b1s[:], b1.rearrange("e (k p) -> p (e k)", p=P)).then_inc(w_in, 16)
                sp.dma_start(w2[:], W2.rearrange("e (k p) c -> p (e k) c", p=P)).then_inc(w_in, 16)
                sp.dma_start(b2s[:], b2.rearrange("e c -> c e")).then_inc(w_in, 16)

            @block.tensor
            def _(pe):
                pe.wait_ge(w_in, 64)
                with pe.Fori(0, NG // 2) as g2:
                    for par in range(2):
                        g = g2 * 2 + par

                        def down_product(j):
                            e, k = divmod(j, KT)
                            pe.wait_ge(relu_done, g * NJ + (j + 3))
                            if k == 0:
                                pe.wait_ge(y_done, g * E + (e + 1))
                            nc.tensor.matmul(po[e % 2][:], w2[:, j], h[:, j % HB], start=(k == 0), stop=(k == KT - 1)).then_inc(down_mm, 1)

                        for j in range(NJ):
                            pe.wait_ge(relu_done, g * NJ + (j + 1))
                            if j % KT == 0:
                                pe.wait_ge(mask_ready, g * E + (j // KT + 1))
                            nc.tensor.matmul(ph[j % 2][:], w1[:, j // KT, (j % KT) * P:(j % KT + 1) * P], XT[:, bass.ds(g * GROUP, GROUP)],
                                             start=True, stop=True).then_inc(up_mm, 1)
                            if j % KT == 0:
                                nc.tensor.matmul(mb[(j // KT) % 2][:], sel[:, j // KT], FT[:, bass.ds(g * GROUP, GROUP)],
                                                 start=True, stop=True).then_inc(mask_mm, 1)
                            if j >= LAG:
                                down_product(j - LAG)
                        for j in range(NJ - LAG, NJ):
                            down_product(j)
                        pe.wait_ge(acc_ready, g + 1)
                        pe.wait_ge(x_added, g + 1)
                        for t in range(TPG):
                            ins = nc.tensor.transpose(tr[par][:, t * P:(t + 1) * P], acc[:, par, t * P:(t + 1) * P], ident[:])
                        ins.then_inc(tr_mm, 1)

            @block.scalar
            def _(act):
                act.wait_ge(w_in, 64)
                act.sem_inc(relu_done, 2)
                act.sem_inc(mask_ready, 2)
                with act.Fori(0, NG // 2) as g2:
                    for par in range(2):
                        g = g2 * 2 + par
                        for j in range(NJ):
                            act.wait_ge(up_mm, g * NJ + (j + 1))
                            act.wait_ge(down_mm, g * NJ + (j + 1))
                            nc.scalar.activation(h[:, j % HB], ph[j % 2][:], ACT.Relu, bias=b1s[:, j:j + 1]).then_inc(relu_done, 1)
                            if j % KT == 1:
                                e = j // KT
                                act.wait_ge(mask_mm, g * E + (e + 1))
                                act.wait_ge(y_done, g * E + (e + 1))
                                nc.scalar.activation(m[:, e % 2], mb[e % 2][:], ACT.Copy).then_inc(mask_ready, 1)

            @block.vector
            def _(dve):
                dve.sem_inc(down_mm, HB)
                dve.sem_inc(y_done, 2)
                dve.sem_inc(x_added, 1)
                dve.wait_ge(w_in, 64)
                with dve.Fori(0, NG // 2) as g2:
                    for par in range(2):
                        g = g2 * 2 + par
                        for e in range(E):
                            dve.wait_ge(mask_ready, g * E + (e + 3))
                            dve.wait_ge(down_mm, g * NJ + ((e + 1) * KT + HB))
                            dst = acc[:, par] if e == 0 else y[:]
                            nc.vector.scalar_tensor_tensor(dst, po[e % 2][:], b2s[:, e:e + 1], m[:, e % 2], ALU.add, ALU.mult).then_inc(y_done, 1)
                            dve.wait_ge(y_done, g * E + (e + 3))
                            if e:
                                ins = nc.vector.tensor_tensor(acc[:, par], acc[:, par], y[:], ALU.add)
                                ins.then_inc(acc_ready if e == E - 1 else acc_chain, 1)
                                if e < E - 1:
                                    dve.wait_ge(acc_chain, g * (E - 2) + e)
                        dve.wait_ge(tr_mm, g + 1)
                        xt = X[:, bass.ds(g * TPG, TPG), :]
                        nc.vector.tensor_tensor(xt, tr[par][:].rearrange("p (t c) -> p t c", c=C), xt, ALU.add).then_inc(x_added, 1)
                dve.wait_ge(x_added, NG + 1)
def delta_rule(nc, X, XN, XT, ident, W_qkvb, W_o, ln_g, ln_b):
    S = BATCH
    D_ = 64
    NH = W_o.shape[1] // D_
    F = 2 * D_
    BUFS = 4
    AHEAD = 3
    ON_DVE = (2, 5)
    XP = D_ + 2
    JT = SEQ // P
    HQ = 4
    HD = NH * D_
    EPS = 1e-5
    SCALE = 1.0 / D_ ** 0.5
    QK = [(s_, S - s_, s_, True) for s_ in range(S)]
    KK = [(s_ + 1, S - 1 - s_, s_, False) for s_ in range(S - 1)]
    GROUPS, row = [], 0
    where = {}
    for t0, n, s_, isq in QK + KK:
        GROUPS.append((t0, n, s_, isq, row))
        for a in range(n):
            where["q" if isq else "k", t0 + a, s_] = row + a
        row += n
    for isq in (True, False):
        for a in range(S):
            where["nq" if isq else "nk", a] = row + a
        row += S
    ROWS = row
    with Stage(nc, "delta") as s:
        wT = s.sb("wT", [P, 3, HD])
        wbT = s.sb("wbT", [P, NH])
        dots = s.sb("dots", [P, ROWS, JT, NH])
        xj = s.sb("xj", [P, 2, S, P])
        apart = s.sem("apart")
        w_go = s.sem("w_go")
        woT = s.sb("woT", [P, HD // P, C])
        with Stage(nc, "wload") as s1:
            NCH = HD // P
            wn = s1.sb("wn", [P, 3, NCH, C])
            wbn = s1.sb("wbn", [NH, C])
            wo_n = s1.sb("wo_n", [P, HD])
            pw = [s1.ps(f"pw{k}") for k in range(8)]
            w_in, w_mm, w_copied = s1.sem("w_in"), s1.sem("w_mm"), s1.sem("w_copied")
            rows = W_qkvb.rearrange("(h o) m -> h o m", o=3 * D_ + 1)
            with nc.Block() as block:

                @block.sync
                def _(sp):
                    for part in range(3):
                        for h2 in range(2):
                            src = rows[:, part * D_:(part + 1) * D_, :].rearrange("(a g) o m -> g o a m", g=2)[h2]
                            sp.dma_start(wn[h2 * D_:(h2 + 1) * D_, part], src).then_inc(w_in, 16)
                    sp.dma_start(wbn[:], rows[:, 3 * D_, :]).then_inc(w_in, 16)
                    sp.dma_start(wo_n[:], W_o).then_inc(w_in, 16)

                @block.tensor
                def _(pe):
                    pe.wait_ge(w_in, 128)
                    for part in range(3):
                        for a in range(NCH):
                            last = nc.tensor.transpose(pw[part * 2 + a // 4][:, (a % 4) * P:(a % 4 + 1) * P], wn[:, part, a], ident[:])
                    nc.tensor.transpose(pw[6][:, 0:NH], wbn[:], ident[0:NH, 0:NH]).then_inc(w_mm, 1)
                    for a in range(NCH):
                        if a == 4:
                            pe.wait_ge(w_copied, 7)
                        last = nc.tensor.transpose(pw[7 if a < 4 else 0][:, (a % 4) * P:(a % 4 + 1) * P], wo_n[:, a * P:(a + 1) * P], ident[:])
                        if a % 4 == 3:
                            last.then_inc(w_mm, 1)

                @block.scalar
                def _(act):
                    act.wait_ge(w_mm, 1)
                    for part in range(3):
                        for half in range(2):
                            nc.scalar.activation(wT[:, part, half * GROUP:(half + 1) * GROUP], pw[part * 2 + half][:], ACT.Copy).then_inc(w_copied, 1)
                    nc.scalar.activation(wbT[:], pw[6][:, 0:NH], ACT.Copy).then_inc(w_copied, 1)
                    for half in range(2):
                        act.wait_ge(w_mm, 2 + half)
                        nc.scalar.activation(woT[:, half * 4:(half + 1) * 4].rearrange("p k c -> p (k c)"), pw[7 if half == 0 else 0][:], ACT.Copy).then_inc(w_copied, 1)
                    act.wait_ge(w_copied, 9)

        XTj = XT[:].rearrange("p (t j n) -> p t j n", t=S, j=JT)

        with Stage(nc, "dots") as s1:
            HH = NH // 2
            x = s1.sb("x", [P, 2, 2, S, HH, XP])
            sg = s1.sb("sg", [P, 2, 2, S, HH, D_], BF16)
            g = s1.sb("g", [P, 2, S, HH, 2, D_])
            ab = s1.sb("ab", [P, 2, HH, 2, D_])
            pr = s1.sb("pr", [P, BUFS, S, HQ, F])
            pu = [s1.ps(f"pu{k}") for k in range(4)]
            xj_ready, u_mm, x_copied, sg_ready, x_ready, ab_ready, g_ready, n_ready, pd_ready, pp_ready, relu_done, d_ready, ab2_ready = (s1.sem(n) for n in (
                "xj_ready", "u_mm", "x_copied", "sg_ready", "x_ready", "ab_ready", "g_ready", "n_ready", "pd_ready", "pp_ready",
                "relu_done", "d_ready", "ab2_ready"))
            FEAT = [(t, a) for t in range(S) for a in range(2)]
            NFE = len(FEAT)
            GA = NFE + 2
            UNITS = [(hq, gr) for hq in range(HH // HQ) for gr in GROUPS]
            NU = len(UNITS)
            on_dve = [k % 7 in ON_DVE for k in range(NU)]
            nd = [sum(on_dve[:k + 1]) for k in range(NU)]
            np_ = [k + 1 - nd[k] for k in range(NU)]
            ND_, NP_ = nd[-1], np_[-1]

            def operands(k):
                hq, (t0, n, s_, isq, _) = UNITS[k]
                hs = slice(hq * HQ, (hq + 1) * HQ)
                a = g[:, 0 if isq else 1, t0:t0 + n, hs].rearrange("p t h a f -> p t h (a f)")
                b = g[:, 1, s_:s_ + 1, hs].rearrange("p t h a f -> p t h (a f)").to_broadcast([P, n, HQ, F])
                return pr[:, k % BUFS, 0:n], a, b

            with nc.Block() as block:

                @block.gpsimd
                def _(pool):
                    def load(j):
                        pool.wait_ge(u_mm, j * 2 * NFE + 1)
                        nc.gpsimd.tensor_copy(xj[:, 0:1].rearrange("p a t n -> p (a t) n").unsqueeze(2), XTj[:, :, bass.ds(j, 1), :]).then_inc(xj_ready, 1)

                    def round_(I, hh):
                        pool.wait_ge(x_ready, I + 1)
                        for k, (t, a) in enumerate(FEAT):
                            pool.wait_ge(g_ready, I * NFE + (k + 1 + NFE))
                            for sh in range(2 - k % 2):
                                ins = nc.gpsimd.tensor_tensor(ab[:, k % 2, :, sh], x[:, hh, a, t, :, 0:D_], x[:, hh, a, t, :, sh + 1:sh + 1 + D_], ALU.mult)
                            ins.then_inc(ab_ready, 1)
                        pool.wait_ge(g_ready, I * NFE + (NFE + GA))
                        for k in range(NU):
                            if not on_dve[k]:
                                pool.wait_ge(d_ready, I * NU + (k + 1))
                                nc.gpsimd.tensor_tensor(*operands(k), ALU.mult).then_inc(pp_ready, 1)

                    load(0)
                    with pool.Fori(0, JT - 1) as j:
                        round_(j * 2, 0)
                        load(j + 1)
                        round_(j * 2 + 1, 1)
                    round_(2 * JT - 2, 0)
                    round_(2 * JT - 1, 1)

                @block.tensor
                def _(pe):
                    pe.sem_inc(u_mm, 1)
                    with pe.Fori(0, JT) as j:
                        pe.wait_ge(xj_ready, j + 1)
                        for hh in range(2):
                            I = j * 2 + hh
                            for k, (t, a) in enumerate(FEAT):
                                pe.wait_ge(sg_ready, I * NFE + (k + 1))
                                nc.tensor.matmul(pu[k % 4][:], xj[:, 0, t], wT[:, a, hh * GROUP:(hh + 1) * GROUP], start=True, stop=True).then_inc(u_mm, 1)

                @block.scalar
                def _(act):
                    def take(I, hh):
                        act.wait_ge(g_ready, I * NFE + 2)
                        for k, (t, a) in enumerate(FEAT):
                            act.wait_ge(u_mm, I * NFE + (k + 2))
                            src = pu[k % 4][:].rearrange("p (h d) -> p h d", d=D_)
                            nc.scalar.activation(x[:, hh, a, t, :, 0:D_], src, ACT.Copy).then_inc(x_copied, 1)
                            nc.scalar.activation(sg[:, hh, a, t], src, ACT.Sign).then_inc(sg_ready, 1)
                        act.wait_ge(x_copied, I * NFE + NFE)
                        nc.scalar.activation(x[:, hh, :, :, :, D_:XP].rearrange("p a t h f -> p (a t h) f"),
                                             x[:, hh, :, :, :, 0:2].rearrange("p a t h f -> p (a t h) f"), ACT.Copy, scale=-1.0).then_inc(x_ready, 1)

                    def clip(I):
                        for k, (hq, (t0, n, s_, isq, _)) in enumerate(UNITS):
                            if on_dve[k]:
                                act.wait_ge(pd_ready, I * ND_ + nd[k])
                            else:
                                act.wait_ge(pp_ready, I * NP_ + np_[k])
                            v_ = pr[:, k % BUFS, 0:n].rearrange("p t h f -> p (t h f)")
                            nc.scalar.activation(v_, v_, ACT.Relu).then_inc(relu_done, 1)

                    act.sem_inc(sg_ready, 4)
                    take(0, 0)
                    with act.Fori(0, JT - 1) as j:
                        for hh in range(2):
                            take(j * 2 + (hh + 1), 1 - hh)
                            clip(j * 2 + hh)
                    take(2 * JT - 1, 1)
                    clip(2 * JT - 2)
                    clip(2 * JT - 1)

                @block.vector
                def _(dve):
                    tt = nc.vector.tensor_tensor
                    dve.sem_inc(g_ready, GA)
                    dve.sem_inc(d_ready, BUFS)
                    dve.sem_inc(n_ready, 1)
                    with dve.Fori(0, JT) as j:
                        for hh in range(2):
                            I = j * 2 + hh
                            dve.wait_ge(d_ready, I * NU + BUFS)
                            dve.wait_ge(n_ready, I * 2 + 1)
                            def second_shift(k):
                                t, a = FEAT[k]
                                dve.wait_ge(g_ready, I * NFE + (k + 1 + NFE))
                                tt(ab[:, 1, :, 1], x[:, hh, a, t, :, 0:D_], x[:, hh, a, t, :, 2:2 + D_], ALU.mult).then_inc(ab2_ready, 1)

                            dve.wait_ge(x_ready, I + 1)
                            for k, (t, a) in enumerate(FEAT):
                                if k % 2 == 0:
                                    second_shift(k + 1)
                                else:
                                    dve.wait_ge(ab2_ready, I * (NFE // 2) + (k + 1) // 2)
                                dve.wait_ge(ab_ready, I * NFE + (k + 1))
                                for sh in range(2):
                                    ins = nc.vector.scalar_tensor_tensor(g[:, a, t, :, sh], ab[:, k % 2, :, sh], 0.0, sg[:, hh, a, t], ALU.max, ALU.mult)
                                ins.then_inc(g_ready, 1)

                            def product(k):
                                if on_dve[k]:
                                    dve.wait_ge(d_ready, I * NU + (k + 1))
                                    tt(*operands(k), ALU.mult).then_inc(pd_ready, 1)

                            dve.wait_ge(g_ready, I * NFE + (NFE + GA))
                            for k in range(AHEAD):
                                product(k)
                            for a, w in ((0, "nq"), (1, "nk")):
                                r0 = where[w, 0]
                                nc.vector.tensor_reduce(dots[:, r0:r0 + S, bass.ds(j, 1), hh * HH:(hh + 1) * HH],
                                                        g[:, a].rearrange("p t h a f -> p t h (a f)").unsqueeze(2),
                                                        AX.X, ALU.add, apply_absolute_value=True).then_inc(n_ready, 1)
                            for k, (hq, (t0, n, s_, isq, r0)) in enumerate(UNITS):
                                h0 = hh * HH + hq * HQ
                                dve.wait_ge(relu_done, I * NU + (k + 1))
                                nc.vector.tensor_reduce(dots[:, r0:r0 + n, bass.ds(j, 1), h0:h0 + HQ], pr[:, k % BUFS, 0:n].unsqueeze(2), AX.X, ALU.add).then_inc(d_ready, 1)
                                if k + AHEAD < NU:
                                    product(k + AHEAD)
                    dve.wait_ge(d_ready, JT * 2 * NU + BUFS)
                    dve.wait_ge(n_ready, 4 * JT + 1)

        alpha = s.sb("alpha", [P, S, S, JT, NH])
        with Stage(nc, "alg") as s1:
            W1 = JT * NH
            beta = s1.sb("beta", [P, S, W1])
            kd = s1.sb("kd", [P, S, W1])
            den = s1.sb("den", [P, S, W1])
            m = s1.sb("m", [P, S, S, W1])
            tmp = s1.sb("tmp", [P, W1])
            acc = s1.sb("acc", [P, W1])
            pb = s1.ps("pb")
            b_mm, b_ready, ch = s1.sem("b_mm"), s1.sem("b_ready"), s1.sem("vector_chain")
            with nc.Block() as block:

                @block.tensor
                def _(pe):
                    for i in range(NT):
                        last = nc.tensor.matmul(pb[:, i * NH:(i + 1) * NH], XT[:, i * P:(i + 1) * P], wbT[:], start=True, stop=True)
                    last.then_inc(b_mm, 1)

                @block.scalar
                def _(act):
                    act.wait_ge(b_mm, 1)
                    nc.scalar.activation(beta[:].rearrange("p t w -> p (t w)"), pb[:], ACT.Sigmoid).then_inc(b_ready, 1)

                @block.vector
                def _(dve):
                    c = Chain(dve, ch)
                    tt, ts = nc.vector.tensor_tensor, nc.vector.tensor_scalar
                    dve.wait_ge(b_ready, 1)
                    c.link(nc.vector.memset(alpha[:], 0.0))

                    def d(*key):
                        return dots[:, where[key]].rearrange("p j h -> p (j h)")

                    def mul(out, a, b):
                        c.link(tt(out, a, b, ALU.mult))

                    def add(out, a, b):
                        c.link(tt(out, a, b, ALU.add))

                    for w in ("nq", "nk"):
                        rows_ = dots[:, where[w, 0]:where[w, 0] + S].rearrange("p t j h -> p (t j h)")
                        c.link(nc.vector.reciprocal(rows_, rows_))
                    def flat(rows_):
                        return rows_.rearrange("p t j h -> p t (j h)")

                    def scale_groups(of_queries, of_keys, keys):
                        for step in range(2):
                            for t0, n, s_, isq, r0 in GROUPS:
                                rows_ = flat(dots[:, r0:r0 + n])
                                by = (of_queries if isq else of_keys)[:, t0:t0 + n] if step == 0 else keys[:, s_:s_ + 1].to_broadcast([P, n, W1])
                                ins = tt(rows_, rows_, by, ALU.mult)
                                ins.then_inc(ch, 1)
                            c.n += len(GROUPS)
                            dve.wait_ge(ch, c.base + c.n)

                    nq = flat(dots[:, where["nq", 0]:where["nq", 0] + S])
                    nk = flat(dots[:, where["nk", 0]:where["nk", 0] + S])
                    scale_groups(nq, nk, nk)
                    c.link(nc.vector.memset(kd[:, 0], 1.0))
                    for t in range(1, S):
                        if t == 1:
                            c.link(nc.vector.tensor_copy(kd[:, 1], d("k", 1, 0)))
                        else:
                            add(kd[:, t], d("k", t, 0), d("k", t, 1))
                            if t == 3:
                                add(kd[:, t], kd[:, t], d("k", t, 2))
                    for t in range(S):
                        if t == 0:
                            c.link(nc.vector.tensor_copy(den[:, 0], d("q", 0, 0)))
                        else:
                            add(den[:, t], d("q", t, 0), d("q", t, 1))
                            for s_ in range(2, t + 1):
                                add(den[:, t], den[:, t], d("q", t, s_))
                    mul(beta[:], beta[:], kd[:])
                    c.link(ts(kd[:], kd[:], EPS, None, ALU.add))
                    c.link(nc.vector.reciprocal(kd[:], kd[:]))
                    c.link(ts(den[:], den[:], EPS, None, ALU.add))
                    c.link(nc.vector.reciprocal(den[:], den[:]))
                    c.link(ts(den[:], den[:], SCALE, None, ALU.mult))
                    scale_groups(den, kd, kd)
                    for t in range(S):
                        c.link(nc.vector.tensor_copy(m[:, t, t], beta[:, t]))
                        for r in range(t):
                            mul(acc[:], d("k", t, r), m[:, r, r])
                            for s_ in range(r + 1, t):
                                mul(tmp[:], d("k", t, s_), m[:, s_, r])
                                add(acc[:], acc[:], tmp[:])
                            mul(acc[:], acc[:], beta[:, t])
                            c.link(ts(m[:, t, r], acc[:], -1.0, None, ALU.mult))
                    for t in range(S):
                        for r in range(t + 1):
                            a = alpha[:, t, r].rearrange("p j h -> p (j h)")
                            mul(a, d("q", t, r), m[:, r, r])
                            for s_ in range(r + 1, t + 1):
                                mul(tmp[:], d("q", t, s_), m[:, s_, r])
                                add(a, a, tmp[:])

        with Stage(nc, "out") as s1:
            v = s1.sb("v", [P, 2, S, NH, D_])
            aj = s1.sb("aj", [P, 2, S, S, NH])
            acc = s1.sb("acc", [P, 2, NH, D_])
            tmp = s1.sb("tmp", [P, 2, NH, D_])
            lT = s1.sb("lT", [P, 2, HD // P, P])
            pv = [s1.ps(f"pv{k}") for k in range(2)]
            pt = [[s1.ps(f"pt{k}{h}") for h in range(2)] for k in range(2)]
            po = [s1.ps(f"po{k}") for k in range(2)]
            xj_ready, aj_ready, v_mm, v_ready, tmp_ready, acc_ready, t_mm, lT_ready, out_mm, x_done, ch, chm = (s1.sem(n) for n in (
                "xj_ready", "aj_ready", "v_mm", "v_ready", "tmp_ready", "acc_ready", "t_mm", "lT_ready", "out_mm", "x_done", "additions", "firsts"))
            NPAIR = S * (S - 1) // 2

            def pipelined(eng, prepare, rest):
                prepare(0, 0)
                with eng.Fori(0, JT // 2 - 1) as j2:
                    for par in range(2):
                        prepare(j2 * 2 + (par + 1), 1 - par)
                        rest(j2 * 2 + par, par)
                prepare(JT - 1, 1)
                rest(JT - 2, 0)
                rest(JT - 1, 1)

            with nc.Block() as block:

                @block.gpsimd
                def _(pool):
                    def prepare(j, par):
                        pool.wait_ge(x_done, j * S + (S + 1))
                        nc.gpsimd.tensor_copy(xj[:, par].unsqueeze(2), XTj[:, :, bass.ds(j, 1), :]).then_inc(xj_ready, 1)
                        nc.gpsimd.tensor_copy(aj[:, par].rearrange("p t s h -> p (t s) h").unsqueeze(2),
                                              alpha[:].rearrange("p t s j h -> p (t s) j h")[:, :, bass.ds(j, 1), :]).then_inc(aj_ready, 1)

                    def rest(j, par):
                        pool.wait_ge(aj_ready, j + 1)
                        k = 0
                        for t in range(1, S):
                            for r in range(1, t + 1):
                                pool.wait_ge(v_ready, j * 2 * S + (2 * r + 4))
                                pool.wait_ge(ch, j * NPAIR + (k + 1))
                                nc.gpsimd.tensor_tensor(tmp[:, k % 2], v[:, par, r], bcast(aj[:, par, t, r], D_), ALU.mult).then_inc(tmp_ready, 1)
                                k += 1

                    pipelined(pool, prepare, rest)

                @block.tensor
                def _(pe):
                    def prepare(j, par):
                        pe.wait_ge(xj_ready, j + 1)
                        for t in range(S):
                            for half in range(2):
                                pe.wait_ge(v_ready, j * 2 * S + (2 * t + half + 1))
                                nc.tensor.matmul(pv[half][:], xj[:, par, t], wT[:, 2, half * GROUP:(half + 1) * GROUP], start=True, stop=True).then_inc(v_mm, 1)

                    def turn(j, t):
                        pe.wait_ge(acc_ready, j * S + (t + 1))
                        for a in range(HD // P):
                            ins = nc.tensor.transpose(pt[t % 2][a // 4][:, (a % 4) * P:(a % 4 + 1) * P],
                                                      acc[:, t % 2].rearrange("p h d -> p (h d)")[:, a * P:(a + 1) * P], ident[:])
                        ins.then_inc(t_mm, 1)

                    def rest(j, par):
                        turn(j, 0)
                        for t in range(S):
                            if t + 1 < S:
                                turn(j, t + 1)
                            pe.wait_ge(lT_ready, j * S + (t + 1))
                            pe.wait_ge(x_done, j * S + (t + 2 * S))
                            for a in range(HD // P):
                                ins = nc.tensor.matmul(po[t % 2][:, 0:C], lT[:, t % 2, a], woT[:, a], start=(a == 0), stop=(a == HD // P - 1))
                            ins.then_inc(out_mm, 1)

                    pipelined(pe, prepare, rest)

                @block.scalar
                def _(act):
                    act.sem_inc(v_ready, 2)
                    def prepare(j, par):
                        act.wait_ge(x_done, j * S + (S + 1))
                        for t in range(S):
                            for half in range(2):
                                act.wait_ge(v_mm, j * 2 * S + (2 * t + half + 1))
                                nc.scalar.activation(v[:, par, t, half * 8:(half + 1) * 8].rearrange("p h d -> p (h d)"), pv[half][:], ACT.Copy).then_inc(v_ready, 1)

                    def rest(j, par):
                        for t in range(S):
                            act.wait_ge(t_mm, j * S + (t + 1))
                            act.wait_ge(x_done, j * S + (t + 2 * S))
                            for half in range(2):
                                ins = nc.scalar.activation(lT[:, t % 2, half * 4:(half + 1) * 4].rearrange("p a n -> p (a n)"), pt[t % 2][half][:], ACT.Copy)
                            ins.then_inc(lT_ready, 1)

                    pipelined(act, prepare, rest)

                @block.vector
                def _(dve):
                    tt = nc.vector.tensor_tensor
                    dve.sem_inc(x_done, 2 * S + 1)
                    dve.sem_inc(ch, 2)
                    with dve.Fori(0, JT // 2) as j2:
                        for par in range(2):
                            j = j2 * 2 + par
                            dve.wait_ge(aj_ready, j + 1)

                            def finish(t):
                                dve.wait_ge(out_mm, j * S + (t + 1))
                                xt = XN[:, bass.ds(j + t * JT, 1), :]
                                tt(xt, po[t % 2][:, 0:C].unsqueeze(1), xt, ALU.add).then_inc(x_done, 1)

                            k = 0
                            for t in range(S):
                                dve.wait_ge(v_ready, j * 2 * S + (2 * t + 4))
                                if t >= 2:
                                    dve.wait_ge(t_mm, j * S + (t - 1))
                                else:
                                    dve.wait_ge(x_done, j * S + (t + 2 * S))
                                ins = tt(acc[:, t % 2], v[:, par, 0], bcast(aj[:, par, t, 0], D_), ALU.mult)
                                if t == 0:
                                    ins.then_inc(acc_ready, 1)
                                else:
                                    ins.then_inc(chm, 1)
                                    dve.wait_ge(chm, j * (S - 1) + t)
                                for r in range(1, t + 1):
                                    dve.wait_ge(tmp_ready, j * NPAIR + (k + 1))
                                    ins = tt(acc[:, t % 2], acc[:, t % 2], tmp[:, k % 2], ALU.add)
                                    ins.then_inc(ch, 1)
                                    k += 1
                                    dve.wait_ge(ch, j * NPAIR + (k + 2))
                                if t:
                                    dve.sem_inc(acc_ready, 1)
                                if t >= 2:
                                    finish(t - 2)
                            finish(S - 2)
                            finish(S - 1)
                    dve.wait_ge(x_done, NT + 2 * S + 1)
    layernorm(nc, XN, XN, None, ident, "ln3")
    with Stage(nc, "fin") as s:
        gb = s.sb("gb", [P, 2, C])
        g_in, ch = s.sem("g_in"), s.sem("vector_chain")
        with nc.Block() as block:

            @block.sync
            def _(sp):
                for k, a in enumerate((ln_g, ln_b)):
                    sp.dma_start(gb[:, k], a.rearrange("(a c) -> a c", a=1).to_broadcast([P, C])).then_inc(g_in, 16)

            @block.vector
            def _(dve):
                c = Chain(dve, ch)
                dve.wait_ge(g_in, 32)
                c.link(nc.vector.tensor_tensor(XN[:], XN[:], gb[:, 0].unsqueeze(1).to_broadcast([P, NT, C]), ALU.mult))
                c.link(nc.vector.tensor_tensor(X[:], X[:], gb[:, 1].unsqueeze(1).to_broadcast([P, NT, C]), ALU.add))
                c.link(nc.vector.tensor_tensor(X[:], X[:], XN[:], ALU.add))
def sinkhorn_gates(nc, XT, ident, gate_w, coef):
    E = gate_w.shape[1]
    TPB = SEQ // P
    TAKEN = SEQ // E
    ITERS = 8
    with Stage(nc, "sink") as s:
        gw = s.sb("gw", [P, E])
        ones = s.sb("ones", [P, P])
        pick = s.sb("pick", [P, E, E], BF16)
        v = s.sb("v", [P, NT, E])
        vb = s.sb("vb", [P, TPB, E])
        col = s.sb("col", [P, BATCH, E])
        row = s.sb("row", [P, NT])
        rowm = s.sb("rowm", [P, NT, 1])
        gb = s.sb("gb", [P, 2, SEQ])
        before = s.sb("before", [P, P])
        ahead = s.sb("ahead", [P, 4, SEQ], BF16)
        cnt = s.sb("cnt", [E, SEQ])
        rank, key, taken = (s.sb(n, [P, NT, E]) for n in ("rank", "key", "taken"))
        number = s.sb("number", [P, E])
        gp = [[s.ps(f"gp{k}{h}") for h in range(2)] for k in range(2)]
        cp = [s.ps(f"cp{h}") for h in range(2)]
        sp_, rp = s.ps("sums"), s.ps("rankT")
        gw_in, made, logits_mm, v_ready, sums_mm, vb_ready, gp_mm, gb_ready, ahead_ready, cnt_mm = (s.sem(n) for n in (
            "gw_in", "made", "logits_mm", "v_ready", "sums_mm", "vb_ready", "gp_mm", "gb_ready", "ahead_ready", "cnt_mm"))
        cnt_copied, rank_mm, rank_ready, ch = (s.sem(n) for n in ("cnt_copied", "rank_mm", "rank_ready", "vector_chain"))
        rank_go = s.sem("rank_go")
        UNITS = E * TPB
        with nc.Block() as block:

            @block.sync
            def _(sp):
                sp.dma_start(gw[:], gate_w).then_inc(gw_in, 16)

            @block.gpsimd
            def _(pool):
                nc.gpsimd.memset(ones[:], 1.0).then_inc(made, 1)
                nc.gpsimd.memset(before[:], LEAST).then_inc(made, 1)
                nc.gpsimd.memset(pick[:], 0.0).then_inc(made, 1)
                pool.wait_ge(made, 3)
                nc.gpsimd.affine_select(out=before[:], in_=before[:], compare_op=ALU.is_gt, fill=0.0, base=0,
                                        pattern=[[1, P]], channel_multiplier=-1).then_inc(made, 1)
                nc.gpsimd.affine_select(out=pick[:], in_=pick[:], compare_op=ALU.not_equal, fill=1.0, base=0,
                                        pattern=[[1, E], [-1, E]], channel_multiplier=0).then_inc(made, 1)
                for e in range(E):
                    nc.gpsimd.memset(number[:, e:e + 1], e + 1.0).then_inc(made, 1)

            @block.tensor
            def _(pe):
                pe.wait_ge(gw_in, 16)
                for i in range(NT):
                    last = nc.tensor.matmul(sp_[:, i * E:(i + 1) * E], XT[:, i * P:(i + 1) * P], gw[:], start=True, stop=True)
                last.then_inc(logits_mm, 1)
                pe.wait_ge(made, 5)
                for it in range(ITERS):
                    pe.wait_ge(v_ready, it + 1)
                    nc.tensor.matmul(sp_[:, 0:NT * E], ones[:], v[:].rearrange("p t e -> p (t e)"), start=True, stop=True).then_inc(sums_mm, 1)
                with pe.Fori(0, BATCH) as b:
                    def spread(e):
                        pe.wait_ge(gb_ready, b * E + (e + 1))
                        for i in range(TPB):
                            ins = nc.tensor.transpose(gp[e % 2][i // TPG][:, (i % TPG) * P:(i % TPG + 1) * P],
                                                      vb[:, i, e:e + 1].to_broadcast([P, P]), ident[:])
                        ins.then_inc(gp_mm, 1)

                    pe.wait_ge(vb_ready, b + 1)
                    spread(0)
                    spread(1)
                    for e in range(E):
                        for i in range(TPB):
                            pe.wait_ge(ahead_ready, b * UNITS + (e * TPB + i + 1))
                            for half in range(2):
                                ins = nc.tensor.matmul(cp[half][0:E, :], pick[:, e], ahead[:, i % 4, half * GROUP:(half + 1) * GROUP],
                                                       start=(e == 0 and i == 0), stop=(e == E - 1 and i == TPB - 1))
                            ins.then_inc(cnt_mm, 1)
                        if e + 2 < E:
                            spread(e + 2)
                    pe.wait_ge(cnt_copied, b + 1)
                    pe.sem_inc(rank_go, 1)
                    for i in range(TPB):
                        ins = nc.tensor.transpose(rp[:, i * E:(i + 1) * E], cnt[:, i * P:(i + 1) * P], ident[0:E, 0:E])
                    ins.then_inc(rank_mm, 1)

            @block.scalar
            def _(act):
                act.sem_inc(gb_ready, 2)
                with act.Fori(0, BATCH) as b:
                    for e in range(E):
                        act.wait_ge(gp_mm, b * E + (e + 1))
                        act.wait_ge(cnt_mm, b * UNITS + (e + 1) * TPB)
                        for half in range(2):
                            ins = nc.scalar.activation(gb[:, e % 2, half * GROUP:(half + 1) * GROUP], gp[e % 2][half][:], ACT.Copy)
                        ins.then_inc(gb_ready, 1)

            @block.vector
            def _(dve):
                c = Chain(dve, ch)
                tt, ts, stt, redu = nc.vector.tensor_tensor, nc.vector.tensor_scalar, nc.vector.scalar_tensor_tensor, nc.vector.tensor_reduce
                dve.wait_ge(logits_mm, 1)
                sums = sp_[:, 0:NT * E]
                ts(v[:], sums.rearrange("p (t e) -> p t e", e=E), 1e-6, None, ALU.max).then_inc(v_ready, 1)
                for it in range(ITERS):
                    dve.wait_ge(sums_mm, it + 1)
                    c.link(redu(col[:], sums.rearrange("p (b t e) -> p b e t", b=BATCH, e=E), AX.X, ALU.add))
                    c.link(nc.vector.reciprocal(col[:], col[:]))
                    v4 = v[:].rearrange("p (b t) e -> p b t e", b=BATCH)
                    c.link(tt(v4, v4, col[:].unsqueeze(2).to_broadcast([P, BATCH, TPB, E]), ALU.mult))
                    c.link(redu(row[:], v[:], AX.X, ALU.add))
                    c.link(nc.vector.reciprocal(row[:], row[:]))
                    tt(v[:], v[:], bcast(row[:], E), ALU.mult).then_inc(v_ready, 1)
                    dve.wait_ge(v_ready, it + 2)
                dve.wait_ge(made, 5 + E)
                dve.sem_inc(cnt_mm, 2 * TPB)
                with dve.Fori(0, BATCH) as b:
                    nc.vector.tensor_copy(vb[:], v[:, bass.ds(b * TPB, TPB), :]).then_inc(vb_ready, 1)
                    dve.wait_ge(vb_ready, b + 1)
                    for e in range(E):
                        dve.wait_ge(gb_ready, b * E + (e + 3))
                        for i in range(TPB):
                            k = e * TPB + i
                            a0, a1, g_i, g_ = i * P, (i + 1) * P, vb[:, i, e:e + 1], gb[:, e % 2]
                            dve.wait_ge(cnt_mm, b * UNITS + (k + 2 * TPB - 3))
                            if i:
                                ts(ahead[:, i % 4, 0:a0], g_[:, 0:a0], g_i, None, ALU.is_lt)
                            if i < TPB - 1:
                                ts(ahead[:, i % 4, a1:], g_[:, a1:], g_i, None, ALU.is_le)
                            stt(ahead[:, i % 4, a0:a1], g_[:, a0:a1], g_i, before[:], ALU.subtract, ALU.is_lt).then_inc(ahead_ready, 1)
                    dve.wait_ge(cnt_mm, b * UNITS + (UNITS + 2 * TPB))
                    for half in range(2):
                        ins = nc.vector.tensor_copy(cnt[:, half * GROUP:(half + 1) * GROUP], cp[half][0:E, :])
                    ins.then_inc(cnt_copied, 1)
                    dve.wait_ge(rank_mm, b + 1)
                    nc.vector.tensor_copy(rank[:, bass.ds(b * TPB, TPB), :], rp[:, 0:TPB * E].rearrange("p (t e) -> p t e", e=E)).then_inc(rank_ready, 1)
                dve.wait_ge(rank_ready, BATCH)
                c.link(ts(taken[:], rank[:], TAKEN - 0.5, None, ALU.is_lt))
                c.link(stt(key[:], rank[:], float(E), number[:].unsqueeze(1).to_broadcast([P, NT, E]), ALU.mult, ALU.add))
                c.link(tt(key[:], key[:], taken[:], ALU.mult))
                c.link(redu(rowm[:], key[:], AX.X, ALU.max))
                c.link(tt(key[:], key[:], rowm[:].to_broadcast([P, NT, E]), ALU.is_equal))
                c.link(tt(key[:], key[:], taken[:], ALU.mult))
                c.link(tt(coef[:], key[:], v[:], ALU.mult))


def sinkhorn_experts(nc, X, XN, XT, ident, gate_w, experts):
    E = experts.shape[0]
    EPB = GROUP // C
    with Stage(nc, "exp") as s:
        coef = s.sb("coef", [P, NT, E])
        w = s.sb("w", [P, E, C])
        xg = s.sb("xg", [P, 2, GROUP])
        w_in = s.sem("w_in")
        sinkhorn_gates(nc, XT, ident, gate_w, coef)
        po = [[s.ps(f"po{k}{h}") for h in range(E // EPB)] for k in range(2)]
        xg_ready, out_mm, x_added, ch = (s.sem(n) for n in ("xg_ready", "out_mm", "x_added", "vector_chain"))
        with nc.Block() as block:

            @block.sync
            def _(sp):
                sp.dma_start(w[:], experts.rearrange("e c f -> c e f")).then_inc(w_in, 16)

            @block.gpsimd
            def _(pool):
                with pool.Fori(0, NG // 2) as g2:
                    for par in range(2):
                        g = g2 * 2 + par
                        pool.wait_ge(out_mm, g * TPG + 1)
                        nc.gpsimd.tensor_copy(xg[:, par], XT[:, bass.ds(g * GROUP, GROUP)]).then_inc(xg_ready, 1)

            @block.tensor
            def _(pe):
                pe.wait_ge(w_in, 16)
                pe.sem_inc(out_mm, TPG + 1)
                with pe.Fori(0, NG // 2) as g2:
                    for par in range(2):
                        g = g2 * 2 + par
                        pe.wait_ge(xg_ready, g + 1)
                        for t in range(TPG):
                            pe.wait_ge(x_added, g * TPG + (t + 1))
                            for h in range(E // EPB):
                                ins = nc.tensor.matmul(po[t % 2][h][:], xg[:, par, t * P:(t + 1) * P],
                                                       w[:, h * EPB:(h + 1) * EPB].rearrange("p e c -> p (e c)"), start=True, stop=True)
                            ins.then_inc(out_mm, 1)

            @block.vector
            def _(dve):
                dve.sem_inc(x_added, 2)
                with dve.Fori(0, NG // 2) as g2:
                    for par in range(2):
                        g = g2 * 2 + par
                        for t in range(TPG):
                            i = g * TPG + t
                            dve.wait_ge(out_mm, g * TPG + (t + TPG + 2))
                            cc = Chain(dve, ch, (g * TPG + t) * (E - 1))
                            xt = X[:, bass.ds(i, 1), :]
                            for e in range(E):
                                o = po[t % 2][e // EPB][:, (e % EPB) * C:(e % EPB + 1) * C].unsqueeze(1)
                                ins = nc.vector.scalar_tensor_tensor(xt, o, coef[:, bass.ds(i, 1), e:e + 1].rearrange("p a b -> p (a b)"), xt, ALU.mult, ALU.add)
                                if e < E - 1:
                                    cc.link(ins)
                                else:
                                    ins.then_inc(x_added, 1)
                dve.wait_ge(x_added, NT + 2)


def program(nc, in_, out):
    s = Stage(nc, "all")
    with s:
        X = s.sb("x", [P, NT, C])
        XN = s.sb("xn", [P, NT, C])
        XT = s.sb("xt", [P, T])
        ident = s.sb("ident", [P, P])
        x_in, made, x_out = s.sem("x_in"), s.sem("made"), s.sem("x_out")
        x_dram = in_["L0_attn_x"].rearrange("b (t p) c -> p (b t) c", p=P)
        out_dram = out.rearrange("b (t p) c -> p (b t) c", p=P)
        with nc.Block() as block:

            @block.sync
            def _(sp):
                sp.dma_start(X[:], x_dram).then_inc(x_in, 16)
                sp.wait_ge(x_in, 16)

            @block.gpsimd
            def _(pool):
                nc.gpsimd.memset(ident[:], 0.0).then_inc(made, 1)
                pool.wait_ge(made, 1)
                nc.gpsimd.affine_select(out=ident[:], in_=ident[:], compare_op=ALU.not_equal, fill=1.0, base=0,
                                        pattern=[[-1, P]], channel_multiplier=1).then_inc(made, 1)
                pool.wait_ge(made, 2)

        def args(prefix, names):
            return [in_[f"{prefix}_{n}"] for n in names.split()]

        RUN = {
            'L0a': lambda: mixer_clipped_scan(nc, X, XN, XT, ident, *args("L0_attn", "in_proj_w A_log B_mat C_mat out_proj_w ln_w ln_b")),
            'L0f': lambda: moe_top2(nc, X, XN, XT, ident, *args("L0_ffn", "gate_w gate_b w1 b1 w2 b2")),
            'L1a': lambda: relu_attention(nc, X, XN, XT, ident, *args("L1_attn", "Wq Wk Wv")),
            'L1f': lambda: moe_grouped(nc, X, XN, XT, ident, *args("L1_ffn", "router_w correction_bias up_w down_w shared_up_w shared_down_w")),
            'L2a': lambda: selective_scan(nc, X, XN, XT, ident, *args("L2_attn", "in_proj_w conv_w conv_b x_proj_w A_log D out_proj_w")),
            'L2f': lambda: moe_capacity(nc, X, XN, XT, ident, *args("L2_ffn", "router_w W1 b1 W2 b2")),
            'L3a': lambda: delta_rule(nc, X, XN, XT, ident, *args("L3_attn", "W_qkvb W_o ln_g ln_b")),
            'L3f': lambda: sinkhorn_experts(nc, X, XN, XT, ident, *args("L3_ffn", "gate_w experts")),
        }
        for name in STAGES:
            layernorm(nc, X, XN, XT if name != 'L0a' else None, ident, f"ln{name}")
            RUN[name]()
        with nc.Block() as block:

            @block.sync
            def _(sp):
                sp.dma_start(out_dram, X[:]).then_inc(x_out, 16)
                sp.wait_ge(x_out, 16)


def kernel(**inputs):
    import numpy as _np
    import concourse.bacc as _bacc
    from concourse import mybir as _mybir
    from concourse.bass_utils import run_bass_kernel_spmd as _run

    nc = _bacc.Bacc("TRN2", target_bir_lowering=False, num_devices=1)
    arrays, in_ = {}, {}
    for name, value in inputs.items():
        a = _np.ascontiguousarray(value)
        arrays[f"in_{name}_dram"] = a
        in_[name] = nc.dram_tensor(f"in_{name}_dram", a.shape, _mybir.dt.from_np(a.dtype), kind="ExternalInput").ap()
    out = nc.dram_tensor("out_dram", inputs["L0_attn_x"].shape, _mybir.dt.from_np(_np.dtype("float32")), kind="ExternalOutput").ap()
    with nc.allow_non_contiguous_dma(reason="small vectors, laid out by channel"):
        program(nc, in_, out)
    r = _run(nc, [arrays], core_ids=[0])
    return r.results[0]["out_dram"]
```
